# Optimizing a Trainium2 kernel written in Bass

```python
import numpy as np
import jax
import jax.numpy as jnp

def _softmax(x, axis=-1):
    return jax.nn.softmax(x, axis=axis)

def _gelu(x):
    return jax.nn.gelu(x, approximate=True)

def _silu(x):
    return jax.nn.silu(x)

def _sigmoid(x):
    return jax.nn.sigmoid(x)

def _layernorm(x, axis=-1, eps=1e-05):
    m = jnp.mean(x, axis=axis, keepdims=True)
    v = jnp.var(x, axis=axis, keepdims=True)
    return (x - m) / jnp.sqrt(v + eps)

def _scatter_add(tgt, idx, src, axis=0):
    return tgt.at[idx].add(src)

def _segment_sum(src, seg, n):
    return jax.ops.segment_sum(src, seg, n)
kernel_name = 'mk_adj_ffn_d1_adj_r2_10da6a'

def setup_inputs(seed: int=0):
    np.random.seed(seed)
    _w = jnp.asarray

    def _rec_inputs():
        import jax
        import jax.numpy as jnp
        _gk = jax.random.key(seed)
        x = -0.0002928 + 1 * jax.random.normal(jax.random.fold_in(_gk, 1), (128, 64, 128), jnp.float32)
        _a = jax.random.bernoulli(jax.random.fold_in(_gk, 2), 0.125, (64, 64))
        _a = jnp.logical_or(_a, jnp.swapaxes(_a, -1, -2))
        _a = jnp.logical_or(_a, jnp.eye(64, dtype=bool))
        adj = _a.astype(jnp.int32)
        return (x, adj)
    x, adj = _rec_inputs()

    def _L0_gnn_setup():
        import jax, jax.numpy as jnp
        import numpy as np
        ALPHA = 0.2
        key = jax.random.key(seed)
        k1, k2, k3, k4 = jax.random.split(key, 4)
        B, N, Din, Dout = (8, 1024, 128, 128)
        h = jax.random.normal(k1, (B, N, Din), dtype=jnp.float32)
        adj = jax.random.randint(k2, (N, N), 0, 2, dtype=jnp.int32)
        w_bound = float(np.sqrt(6.0 / (Din + Dout)))
        a_bound = float(np.sqrt(6.0 / (2 * Dout + 1)))
        W = jax.random.uniform(k3, (Din, Dout), dtype=jnp.float32, minval=-w_bound, maxval=w_bound)
        a = jax.random.uniform(k4, (2 * Dout, 1), dtype=jnp.float32, minval=-a_bound, maxval=a_bound)
        return {'h': h, 'adj': adj, 'W': W, 'a': a}
    _L0_gnn_all = _L0_gnn_setup()
    _L0_gnn_in = {k: v for k, v in _L0_gnn_all.items() if k in ('W', 'a')}
    del _L0_gnn_all

    def _L0_ffn_setup():
        import jax, jax.numpy as jnp
        import numpy as np
        B, S, D, H, E, K = (8, 4096, 128, 512, 8, 2)
        key = jax.random.key(seed)
        ks = jax.random.split(key, 7)
        s_in = 1.0 / np.sqrt(D)
        s_hid = 1.0 / np.sqrt(H)
        return {'x': jax.random.normal(ks[0], (B, S, D), dtype=jnp.float32), 'Wg': jax.random.uniform(ks[1], (E, D), jnp.float32, -s_in, s_in), 'bg': jax.random.uniform(ks[2], (E,), jnp.float32, -s_in, s_in), 'W1': jax.random.uniform(ks[3], (E, H, D), jnp.float32, -s_in, s_in), 'b1': jax.random.uniform(ks[4], (E, H), jnp.float32, -s_in, s_in), 'W2': jax.random.uniform(ks[5], (E, D, H), jnp.float32, -s_hid, s_hid), 'b2': jax.random.uniform(ks[6], (E, D), jnp.float32, -s_hid, s_hid)}
    _L0_ffn_all = _L0_ffn_setup()
    _L0_ffn_in = {k: v for k, v in _L0_ffn_all.items() if k in ('Wg', 'bg', 'W1', 'b1', 'W2', 'b2')}
    del _L0_ffn_all
    return {'x': x, 'adj': adj, 'L0_gnn_W': _L0_gnn_in['W'], 'L0_gnn_a': _L0_gnn_in['a'], 'L0_ffn_Wg': _L0_ffn_in['Wg'], 'L0_ffn_bg': _L0_ffn_in['bg'], 'L0_ffn_W1': _L0_ffn_in['W1'], 'L0_ffn_b1': _L0_ffn_in['b1'], 'L0_ffn_W2': _L0_ffn_in['W2'], 'L0_ffn_b2': _L0_ffn_in['b2']}

def reference(x, adj, L0_gnn_W, L0_gnn_a, L0_ffn_Wg, L0_ffn_bg, L0_ffn_W1, L0_ffn_b1, L0_ffn_W2, L0_ffn_b2):
    import jax
    import jax.numpy as jnp

    def _L0_gnn_ref(h, adj, W, a):
        import jax, jax.numpy as jnp
        import numpy as np
        ALPHA = 0.2
        Wh = jnp.matmul(h, W)
        D = W.shape[1]
        e_src = jnp.matmul(Wh, a[:D])
        e_dst = jnp.matmul(Wh, a[D:])
        e = e_src + jnp.swapaxes(e_dst, 1, 2)
        e = jnp.where(e > 0, e, ALPHA * e)
        mask = (adj > 0)[None, :, :]
        e = jnp.where(mask, e, -jnp.inf)
        alpha_w = jax.nn.softmax(e, axis=-1)
        h_prime = jnp.matmul(alpha_w, Wh)
        return jax.nn.elu(h_prime)

    def _L0_ffn_ref(x, Wg, bg, W1, b1, W2, b2):
        import jax, jax.numpy as jnp
        import numpy as np
        B, S, D, H, E, K = (8, 4096, 128, 512, 8, 2)
        gate_scores = jnp.einsum('bsd,ed->bse', x, Wg) + bg
        topk_scores, topk_idx = jax.lax.top_k(gate_scores, K)
        topk_probs = jax.nn.softmax(topk_scores, axis=-1)
        combine = jnp.sum(topk_probs[..., None] * jax.nn.one_hot(topk_idx, E, dtype=x.dtype), axis=-2)
        out = jnp.zeros_like(x)
        for e in range(E):
            h = jax.nn.relu(jnp.einsum('bsd,hd->bsh', x, W1[e]) + b1[e])
            y = jnp.einsum('bsh,dh->bsd', h, W2[e]) + b2[e]
            out = out + combine[..., e:e + 1] * y
        return out
    x = x + _L0_gnn_ref(_layernorm(x, axis=-1), adj, L0_gnn_W, L0_gnn_a)
    x = x + _L0_ffn_ref(_layernorm(x, axis=-1), L0_ffn_Wg, L0_ffn_bg, L0_ffn_W1, L0_ffn_b1, L0_ffn_W2, L0_ffn_b2)
    return x

_drawn_inputs = setup_inputs


def setup_inputs(seed=0):
    import zlib

    import numpy as np

    out = dict(_drawn_inputs(seed))
    spreads = {}
    factors = {'L0_ffn_b1': 4.006, 'L0_ffn_b2': 3.186}
    for name, (base, spread) in spreads.items():
        noise = np.random.default_rng([zlib.crc32(name.encode()), seed]).standard_normal(out[name].shape)
        drawn = base * np.exp(spread * noise) if base else spread * noise
        out[name] = jnp.asarray(drawn.astype(out[name].dtype))
    for name, factor in factors.items():
        out[name] = (out[name] * factor).astype(out[name].dtype)
    return out
```

```python
import concourse.bass as bass
from concourse import mybir
from contextlib import ExitStack

F32 = mybir.dt.float32
F32R = mybir.dt.float32r
BF16 = mybir.dt.bfloat16
I32 = mybir.dt.int32
U32 = mybir.dt.uint32
ALU = mybir.AluOpType
ACT = mybir.ActivationFunctionType
AX = mybir.AxisListType.X

P = 128
NODES = 64
TOKENS = 128 * NODES
D = 128
H = 512
E = 8
SUB = 4
GROUP = SUB * P
GROUPS = TOKENS // GROUP
HC = H // P
ROW = D + E + 1
ID = D + E
CAP = TOKENS + GROUP
EPS = 1e-5
SLOPE = 0.2
STAGES = 5
MASKED = -1e30
FIRST = 1

C_IDENT = 0
C_BEFORE = C_IDENT + P
C_EXPERT = C_BEFORE + P
C_BASE = C_EXPERT + 2 * SUB * E
C_TOKEN = C_BASE + SUB * E
C_PAD = C_TOKEN + SUB
C_END = C_PAD + SUB


def shape_constants(np):
    c = np.zeros((P, C_END), np.float32)
    c[:, C_IDENT:C_IDENT + P] = np.eye(P)
    c[:, C_BEFORE:C_BEFORE + P] = np.triu(np.ones((P, P)), 1)
    c[:, C_EXPERT:C_BASE] = np.tile(np.arange(E), 2 * SUB)
    c[:, C_BASE:C_TOKEN] = np.tile(np.arange(E) * CAP, SUB)
    c[:, C_TOKEN:C_PAD] = np.arange(SUB)[None, :] * P + np.arange(P)[:, None]
    c[:, C_PAD:C_END] = TOKENS + np.arange(P)[:, None] * SUB + np.arange(SUB)[None, :]
    return c


def gnn_moe_kernel(nc, x, adj, w, wt, a, wg_t, bg, w1_t, b1_t, w2_t, b2_t, consts, out):
    ctx = ExitStack()
    with ctx:
        def sb(name, shape, dt=F32):
            return ctx.enter_context(nc.sbuf_tensor(name, shape, dt))

        def sem(name):
            return ctx.enter_context(nc.semaphore(name))

        slots = nc.dram_tensor("expert_slots", [E * CAP, ROW], F32, kind="Internal").ap()
        x_groups = x.rearrange("(g s p) d -> g p s d", s=SUB, p=P)
        out_groups = out[0:TOKENS, :].rearrange("(g s p) d -> g p s d", s=SUB, p=P)

        cst = sb("cst", [P, C_END])
        ident = cst[:, C_IDENT:C_IDENT + P]
        expert_no = cst[:, C_EXPERT:C_BASE].rearrange("p (k s e) -> p k s e", k=2, s=SUB)
        ident_b = sb("ident_b", [P, P], BF16)
        before_b = sb("before_b", [P, P], BF16)
        ones_b = sb("ones_b", [P, P], BF16)
        minus_half = sb("minus_half", [P, 2 * SUB])
        act_scratch = sb("act_scratch", [P, 1])
        pool_scratch = sb("pool_scratch", [P, 1])
        w_sb = sb("w_sb", [P, D])
        wt_sb = sb("wt_sb", [P, D])
        a_sb = sb("a_sb", [P, 2])
        a_rep = sb("a_rep", [P, 2, P])
        w_a = sb("w_a", [P, 2, P])
        adj_i = sb("adj_i", [P, P], I32)
        mask_b = sb("mask_b", [P, SUB, P], BF16)
        wg_sb = sb("wg_sb", [P, E])
        bg_sb = sb("bg_sb", [P, E])
        b1_sb = sb("b1_sb", [P, E, HC])
        b2_sb = sb("b2_sb", [P, E])
        w1_raw = sb("w1_raw", [P, E, H])
        w2_raw = sb("w2_raw", [P, E, HC, D])
        w1_hi = sb("w1_hi", [P, E, H], F32R)
        w1_lo = sb("w1_lo", [P, E, H], F32R)
        w2_hi = sb("w2_hi", [P, E, HC, D], F32R)
        w2_lo = sb("w2_lo", [P, E, HC, D], F32R)
        pad_rows = sb("pad_rows", [P, SUB, ROW])

        x_all = sb("x_all", [P, GROUPS, SUB, D])
        bn = sb("bn", [P, 2, SUB, 6])
        mv = sb("mv", [P, 2, SUB, 2])
        var_eps = sb("var_eps", [P, 2 * SUB])
        rstd = sb("rstd", [P, 2 * SUB])
        xn1 = sb("xn1", [P, SUB, D])
        xn1_t = sb("xn1_t", [P, GROUP])
        z = sb("z", [P, SUB, P])
        wh = [sb(f"wh{q}", [P, SUB, D]) for q in range(2)]
        score = sb("score", [P, SUB, P])
        smax = sb("smax", [P, SUB])
        neg_max = sb("neg_max", [P, SUB])
        prob = sb("prob", [P, SUB, P])
        psum_row = sb("psum_row", [P, SUB])
        prob_t = sb("prob_t", [P, SUB, P])
        inv_sum = sb("inv_sum", [P, SUB])
        hn = sb("hn", [P, SUB, D])
        hmin = sb("hmin", [P, SUB, D])
        hexp = sb("hexp", [P, SUB, D])
        helu = sb("helu", [P, SUB, D])
        x2 = [sb(f"x2_{q}", [P, SUB, D]) for q in range(2)]
        xn2 = sb("xn2", [P, SUB, D])
        rows = [sb(f"rows{q}", [P, SUB, ROW]) for q in range(2)]
        xn2_t = sb("xn2_t", [P, GROUP])
        logit = sb("logit", [P, SUB, E])
        top = sb("top", [P, SUB, 8])
        top_i = sb("top_i", [P, SUB, 8], U32)
        gap = sb("gap", [P, SUB])
        gap_e = sb("gap_e", [P, SUB])
        gap_1 = sb("gap_1", [P, SUB])
        top_f = sb("top_f", [P, 2, SUB])
        gate_p = sb("gate_p", [P, 2, SUB])
        chosen = sb("chosen", [P, 2, SUB, E])
        weighed = sb("weighed", [P, 2, SUB, E])
        chosen_b = sb("chosen_b", [P, SUB, E], BF16)
        seen_b = sb("seen_b", [P, SUB + 1, E], BF16)
        rank = sb("rank", [P, SUB, E])
        slot_p = sb("slot_p", [P, 2, SUB, E])
        slot_i = [sb(f"slot_i{q}", [P, 2 * SUB], I32) for q in range(2)]
        token_f = sb("token_f", [P, SUB])
        count_f = sb("count_f", [P, E])
        count_i = sb("count_i", [P, E], I32)
        blocks_f = sb("blocks_f", [P, E])
        blocks_i = sb("blocks_i", [P, E], I32)
        blocks_r = sb("blocks_r", [P, E])
        blocks_m = sb("blocks_m", [P, E])
        ones8 = sb("ones8", [P, E])
        until_f = sb("until_f", [P, E])
        until_i = sb("until_i", [P, E], I32)

        xs = sb("xs", [P, SUB, ROW])
        xh = sb("xh", [P, GROUP], F32R)
        xl = sb("xl", [P, GROUP], F32R)
        meta = sb("meta", [P, SUB, E + 1])
        wgt = sb("wgt", [P, 2, SUB])
        tid = sb("tid", [P, 2, SUB], I32)
        hr = w1_raw[:, 0:HC, :]
        hh = sb("hh", [P, HC, GROUP], F32R)
        hl = sb("hl", [P, HC, GROUP], F32R)
        yb = sb("yb", [P, GROUP])
        ys = [sb(f"ys{s}", [P, D]) for s in range(SUB)]
        ysi = [sb(f"ysi{s}", [P, 1], I32) for s in range(SUB)]

        bank = [ctx.enter_context(nc.psum_tensor(f"bank{n}", [P, 512], F32)) for n in range(8)]
        ps_t1, ps_z, ps_wh, ps_tp, ps_av, ps_t3, ps_route, ps_setup = bank
        ps_gate, ps_rank, ps_count = ps_route[:, 0:SUB * E], ps_setup[:, 0:SUB * E], ps_setup[:, 64:64 + E]
        ps_h = bank[0:4]
        ps_x, ps_y, ps_yt = bank[4:7]

        c_w = sem("c_w")
        c_wt = sem("c_wt")
        c_a = sem("c_a")
        c_adj0 = sem("c_adj0")
        c_adj1 = sem("c_adj1")
        c_cst = sem("c_cst")
        c_wg = sem("c_wg")
        c_bg = sem("c_bg")
        c_b1 = sem("c_b1")
        c_b2 = sem("c_b2")
        c_w1 = sem("c_w1")
        c_w2 = sem("c_w2")
        int_zeros = sem("int_zeros")
        row_zeros = sem("row_zeros")
        start_ok = sem("start_ok")
        a_rep_ok = sem("a_rep_ok")
        wa_ps = sem("wa_ps")
        wa_ok = sem("wa_ok")
        mask_ok = sem("mask_ok")
        pads_ok = sem("pads_ok")
        hi_ok = sem("hi_ok")
        lo_ok = sem("lo_ok")
        stats_ok = sem("stats_ok")
        aggr_ok = sem("aggr_ok")
        var_ok = sem("var_ok")
        rstd_ok = sem("rstd_ok")
        xn1_ok = sem("xn1_ok")
        xn1_ps = sem("xn1_ps")
        xn1_t_ok = sem("xn1_t_ok")
        z_ps = sem("z_ps")
        wh_ps = sem("wh_ps")
        z_ok = sem("z_ok")
        wh_ok = sem("wh_ok")
        score_ok = sem("score_ok")
        max_ok = sem("max_ok")
        neg_ok = sem("neg_ok")
        exp_ok = sem("exp_ok")
        prob_ps = sem("prob_ps")
        prob_t_ok = sem("prob_t_ok")
        av_ps = sem("av_ps")
        inv_ok = sem("inv_ok")
        hn_ok = sem("hn_ok")
        min_ok = sem("min_ok")
        hexp_ok = sem("hexp_ok")
        helu_ok = sem("helu_ok")
        x2_ok = sem("x2_ok")
        xn2_ok = sem("xn2_ok")
        xn2_ps = sem("xn2_ps")
        xn2_t_ok = sem("xn2_t_ok")
        gate_ps = sem("gate_ps")
        logit_ok = sem("logit_ok")
        top_ok = sem("top_ok")
        topi_ok = sem("topi_ok")
        gap_ok = sem("gap_ok")
        gape_ok = sem("gape_ok")
        gap1_ok = sem("gap1_ok")
        topf_ok = sem("topf_ok")
        p1_ok = sem("p1_ok")
        p2_ok = sem("p2_ok")
        chosen_ok = sem("chosen_ok")
        weighed_ok = sem("weighed_ok")
        chosenb_ok = sem("chosenb_ok")
        rowid_ok = sem("rowid_ok")
        rowx_ok = sem("rowx_ok")
        rowp_ok = sem("rowp_ok")
        seen_ok = sem("seen_ok")
        rank_ps = sem("rank_ps")
        rank_ok = sem("rank_ok")
        slotp_ok = sem("slotp_ok")
        token_ok = sem("token_ok")
        slot_ok = sem("slot_ok")
        count_ps = sem("count_ps")
        count_ok = sem("count_ok")
        blocks_ok = sem("blocks_ok")
        table_ok = sem("table_ok")
        pads_out = sem("pads_out")
        xs_in = sem("xs_in")
        xs_ps = sem("xs_ps")
        xh_ok = sem("xh_ok")
        xl_ok = sem("xl_ok")
        meta_ok = sem("meta_ok")
        own_ok = sem("own_ok")
        h_ps = sem("h_ps")
        r_ok = sem("r_ok")
        hh_ok = sem("hh_ok")
        hl_ok = sem("hl_ok")
        y_ps = sem("y_ps")
        yb_ok = sem("yb_ok")
        yt_ps = sem("yt_ps")
        ys_ok = sem("ys_ok")
        dump_ok = sem("dump_ok")
        stood = sem("stood")
        x_in, rows_out, stored = ([sem(f"{n}{q}") for q in range(2)] for n in ("x_in", "rows_out", "stored"))
        added = [sem(f"added{t}") for t in range(SUB)]

        def later(n):
            return not isinstance(n, int) or n > 0

        def by_steps(eng, step):
            def at(t):
                step(t, [t - n if 0 <= t - n < GROUPS else None for n in range(STAGES)], t % 2, t // 2)

            for t in range(6):
                at(t)
            with eng.Fori(3, GROUPS // 2) as m:
                for q in range(2):
                    step(2 * m + q, [2 * m + (q - n) for n in range(STAGES)], q, m)
            for t in range(GROUPS, GROUPS + STAGES - 1):
                at(t)

        def block_bounds(eng):
            eng.wait_ge(table_ok, 1)
            return [0] + [eng.value_load(until_i[0:1, e:e + 1], min_val=1, max_val=TOKENS * 2 // GROUP + E)
                          for e in range(E)]

        block = ctx.enter_context(nc.Block())

        @block.sync
        def _(sp):
            sp.dma_start(cst[:, :], consts).then_inc(c_cst, 16)
            sp.dma_start(wt_sb[:, :], wt).then_inc(c_wt, 16)
            sp.dma_start(a_sb[:, :], a).then_inc(c_a, 16)
            for g in range(2):
                sp.dma_start(x_all[:, g, :, :], x_groups[g]).then_inc(x_in[g % 2], 16)
            sp.dma_start(w_sb[:, :], w).then_inc(c_w, 16)
            sp.wait_ge(int_zeros, 1)
            sp.dma_start(adj_i[0:NODES, 0:NODES], adj).then_inc(c_adj0, 16)
            sp.dma_start(adj_i[NODES:P, NODES:P], adj).then_inc(c_adj1, 16)
            sp.dma_start(wg_sb[:, :], wg_t).then_inc(c_wg, 16)
            sp.dma_start(bg_sb[:, :], bg.partition_broadcast(P)).then_inc(c_bg, 16)
            with sp.Fori(1, GROUPS // 2) as m:
                for q in range(2):
                    sp.wait_ge(x_in[q], 16 * m)
                    sp.dma_start(x_all[:, bass.ds(2 * m + q, 1), :, :],
                                 x_groups[bass.ds(2 * m + q, 1)].rearrange("g p s d -> p g s d")).then_inc(x_in[q], 16)
            sp.dma_start(b1_sb[:, :, :], b1_t).then_inc(c_b1, 16)
            sp.dma_start(b2_sb[:, :], b2_t).then_inc(c_b2, 16)
            sp.wait_ge(pads_ok, 1)
            sp.dma_start(out[TOKENS:TOKENS + GROUP, :].rearrange("(p s) d -> p s d", s=SUB),
                         pad_rows[:, :, 0:D]).then_inc(dump_ok, 16)
            with sp.Fori(0, GROUPS // 2) as m:
                for q in range(2):
                    sp.wait_ge(x2_ok, 2 * m + (q + 1))
                    sp.dma_start(out_groups[bass.ds(2 * m + q, 1)].rearrange("g p s d -> p g s d"),
                                 x2[q][:, :, :].rearrange("p (g s) d -> p g s d", g=1)).then_inc(stored[q], 16)
            sp.wait_ge(table_ok, 1)
            for e in range(E):
                n = sp.value_load(count_i[0:1, e:e + 1], min_val=0, max_val=TOKENS)
                sp.dma_start(slots[bass.ds(n + e * CAP, GROUP), :].rearrange("(p s) r -> p s r", s=SUB),
                             pad_rows[:, :, :]).then_inc(pads_out, 16)
            bounds = block_bounds(sp)
            sp.wait_ge(pads_out, 16 * E)
            for q in range(2):
                sp.wait_ge(rows_out[q], 16 * 2 * SUB * (GROUPS // 2))

            def load_block(first_row, i):
                sp.wait_ge(xs_ps, i + FIRST)
                sp.wait_ge(meta_ok, i + FIRST)
                sp.dma_start(xs[:, :, :], slots[bass.ds(first_row, GROUP), :].rearrange("(p s) r -> p s r", s=SUB)
                             ).then_inc(xs_in, 16)

            for e in range(E):
                with sp.Fori(bounds[e], bounds[e + 1]) as i:
                    row = nc.s_assert_within((i - bounds[e]) * GROUP + e * CAP, e * CAP, (e + 1) * CAP - GROUP,
                                             skip_runtime_bounds_check_because="an expert has at most TOKENS tokens")
                    load_block(row, i)
            load_block(0, bounds[E])
            for q in range(2):
                sp.wait_ge(stored[q], 16 * (GROUPS // 2))

        def stand(pool, before):
            pool.wait_ge(stood, before + FIRST)
            nc.gpsimd.tensor_tensor(pool_scratch[:, :], minus_half[:, 0:1], minus_half[:, 0:1], ALU.add
                                    ).then_inc(stood, 1)

        @block.gpsimd
        def _(pool):
            nc.gpsimd.memset(adj_i[:, :], 0).then_inc(int_zeros, 1)
            nc.gpsimd.memset(minus_half[:, :], -0.5).then_inc(stood, FIRST)
            nc.gpsimd.memset(pad_rows[:, :, :], 0.0).then_inc(row_zeros, 1)
            pool.wait_ge(c_cst, 16)
            pool.wait_ge(row_zeros, 1)
            nc.gpsimd.tensor_copy(pad_rows[:, :, ID].bitcast(I32), cst[:, C_PAD:C_END]).then_inc(pads_ok, 1)
            pool.wait_ge(c_w1, 16)
            pool.wait_ge(c_w2, 16)
            raws = [w1_raw[:, :, :].rearrange("p e h -> p (e h)"), w2_raw[:, :, :, :].rearrange("p e c d -> p (e c d)")]
            his = [w1_hi[:, :, :].rearrange("p e h -> p (e h)"), w2_hi[:, :, :, :].rearrange("p e c d -> p (e c d)")]
            los = [w1_lo[:, :, :].rearrange("p e h -> p (e h)"), w2_lo[:, :, :, :].rearrange("p e c d -> p (e c d)")]

            def step(t, groups, q, m):
                g1, _, g3, _, g5 = groups
                if g1 is not None or g3 is not None:
                    pool.wait_ge(var_ok, t + 1)
                    nc.gpsimd.tensor_tensor(rstd[:, :], var_eps[:, :], minus_half[:, :], ALU.pow).then_inc(rstd_ok, 1)
                if isinstance(t, int) and t < 4:
                    part = slice((t % 2) * E * H // 2, (t % 2 + 1) * E * H // 2)
                    nc.gpsimd.tensor_copy(his[t // 2][:, part], raws[t // 2][:, part]).then_inc(hi_ok, 1)
                    pool.wait_ge(hi_ok, t + 1)
                    nc.gpsimd.tensor_tensor(los[t // 2][:, part], raws[t // 2][:, part], his[t // 2][:, part].bitcast(F32),
                                            ALU.subtract).then_inc(lo_ok, 1)
                if g5 is not None:
                    pool.wait_ge(slot_ok, g5 + 1)
                    pool.wait_ge(rowx_ok, g5 + 1)
                    stand(pool, g5)
                    for k in range(2):
                        for j in range(SUB):
                            nc.gpsimd.indirect_dma_start(
                                out=slots, out_offset=bass.IndirectOffsetOnAxis(
                                    ap=slot_i[q][:, k * SUB + j:k * SUB + j + 1], axis=0),
                                in_=rows[q][:, j, :], in_offset=None).then_inc(rows_out[q], 16)

            by_steps(pool, step)
            bounds = block_bounds(pool)
            for q in range(2):
                pool.wait_ge(stored[q], 16 * (GROUPS // 2))
            pool.wait_ge(dump_ok, 16)

            def add_rows(i, experts):
                for t in range(SUB):
                    if t % 2 == 0:
                        pool.wait_ge(ys_ok, 2 * (i + 1) + (FIRST + 1 + t // 2))
                        stand(pool, GROUPS + experts + 2 * (i + 1) + t // 2)
                    nc.gpsimd.indirect_dma_start(
                        out=out, out_offset=bass.IndirectOffsetOnAxis(ap=ysi[t][:, :], axis=0),
                        in_=ys[t][:, :], in_offset=None, compute_op=ALU.add).then_inc(added[t], 16)

            add_rows(-1, 0)
            for e in range(E):
                for t in range(SUB):
                    pool.wait_ge(added[t], bounds[e] * 16 + 16)
                stand(pool, GROUPS + e + 2 * (bounds[e] + 1))
                with pool.Fori(bounds[e], bounds[e + 1]) as i:
                    add_rows(i, e + 1)
            for t in range(SUB):
                pool.wait_ge(added[t], bounds[E] * 16 + 16)

        @block.scalar
        def _(act):
            act.dma_start(w1_raw[:, :, :], w1_t).then_inc(c_w1, 16)
            act.dma_start(w2_raw[:, :, :, :], w2_t).then_inc(c_w2, 16)
            act.wait_ge(c_cst, 16)
            nc.scalar.copy(act_scratch[:, :], cst[:, 0:1]).then_inc(yb_ok, FIRST)
            act.wait_ge(wa_ps, 1)
            nc.scalar.copy(w_a[:, :, :], ps_setup[:, 0:2 * P].rearrange("p (k j) -> p k j", k=2)).then_inc(wa_ok, 1)

            def step(t, groups, q, m):
                g1, g2, g3, g4, _ = groups
                if g2 is not None:
                    act.wait_ge(neg_ok, g2 + 1)
                    if later(g2):
                        act.wait_ge(prob_ps, g2)
                    for j in range(SUB):
                        last = nc.scalar.activation(prob[:, j, :], score[:, j, :], ACT.Exp, bias=neg_max[:, j:j + 1],
                                                    accum_out=psum_row[:, j:j + 1])
                    last.then_inc(exp_ok, 1)
                if g4 is not None:
                    act.wait_ge(gap_ok, g4 + 1)
                    nc.scalar.activation(gap_e[:, :], gap[:, :], ACT.Exp).then_inc(gape_ok, 1)
                if g2 is not None:
                    act.wait_ge(prob_ps, g2 + 1)
                    if later(g2):
                        act.wait_ge(av_ps, g2)
                    nc.scalar.copy(prob_t[:, :, :], ps_tp[:, :].rearrange("p (t j) -> p t j", t=SUB)).then_inc(prob_t_ok, 1)
                if g4 is not None:
                    if later(m + (q - 2)):
                        act.wait_ge(rows_out[1 - q], 16 * 2 * SUB * (m + (q - 2)))
                    act.wait_ge(xn2_ok, g4 + 1)
                    nc.scalar.copy(rows[1 - q][:, :, 0:D], xn2[:, :, :]).then_inc(rowx_ok, 1)
                if g1 is not None:
                    act.wait_ge(xn1_ps, g1 + 1)
                    nc.scalar.copy(xn1_t[:, :], ps_t1[:, :]).then_inc(xn1_t_ok, 1)
                if g3 is not None:
                    act.wait_ge(xn2_ps, g3 + 1)
                    nc.scalar.copy(xn2_t[:, :], ps_t3[:, :]).then_inc(xn2_t_ok, 1)
                if g2 is not None:
                    act.wait_ge(min_ok, g2 + 1)
                    nc.scalar.activation(hexp[:, :, :], hmin[:, :, :], ACT.Exp).then_inc(hexp_ok, 1)
                if g1 is not None:
                    act.wait_ge(z_ps, g1 + 1)
                    if later(g1):
                        act.wait_ge(score_ok, g1)
                    nc.scalar.copy(z[:, :, :], ps_z[:, :].rearrange("p (t j) -> p t j", t=SUB)).then_inc(z_ok, 1)
                    act.wait_ge(wh_ps, g1 + 1)
                    if later(g1 - 1):
                        act.wait_ge(av_ps, g1 - 1)
                    nc.scalar.copy(wh[q][:, :, :], ps_wh[:, :].rearrange("p (t j) -> p t j", t=SUB)).then_inc(wh_ok, 1)

            by_steps(act, step)
            bounds = block_bounds(act)
            act.wait_ge(c_b1, 16)
            act.wait_ge(c_b2, 16)

            def round_x(i):
                act.wait_ge(xs_ps, i + FIRST + 1)
                nc.scalar.copy(xh[:, :], ps_x[:, :]).then_inc(xh_ok, 1)

            round_x(0)
            for e in range(E):
                with act.Fori(bounds[e], bounds[e + 1]) as i:
                    for c in range(HC):
                        act.wait_ge(h_ps, HC * i + (c + 1))
                        nc.scalar.activation(hr[:, c, :], ps_h[c][:, :], ACT.Relu, bias=b1_sb[:, e, c:c + 1]
                                             ).then_inc(r_ok, 1)
                    round_x(i + 1)
                    act.wait_ge(y_ps, i + 1)
                    nc.scalar.activation(yb[:, :], ps_y[:, :], ACT.Identity, bias=b2_sb[:, e:e + 1]
                                         ).then_inc(yb_ok, 1)

        @block.vector
        def _(dve):
            nc.vector.memset(ones_b[:, :], 1.0)
            nc.vector.memset(ones8[:, :], 1.0).then_inc(meta_ok, FIRST)
            nc.vector.memset(yb[:, :], 0.0).then_inc(ys_ok, FIRST)
            nc.vector.memset(wgt[:, :, :], 0.0).then_inc(own_ok, FIRST)
            nc.vector.memset(mv[:, :, :, :], 1.0)
            nc.vector.memset(seen_b[:, :, :], 0.0).then_inc(start_ok, 1)
            dve.wait_ge(c_cst, 16)
            nc.vector.tensor_copy(ident_b[:, :], ident)
            nc.vector.tensor_copy(before_b[:, :], cst[:, C_BEFORE:C_BEFORE + P])
            nc.vector.tensor_copy(token_f[:, :], cst[:, C_TOKEN:C_PAD])
            for k in range(2):
                nc.vector.tensor_copy(tid[:, k, :], cst[:, C_PAD:C_END])
            dve.wait_ge(start_ok, 1)
            dve.wait_ge(c_a, 16)
            for k in range(2):
                last = nc.vector.tensor_scalar(a_rep[:, k, :], ones_b[:, :], a_sb[:, k:k + 1], None, ALU.mult)
            last.then_inc(a_rep_ok, 1)
            dve.wait_ge(c_adj0, 16)
            dve.wait_ge(c_adj1, 16)
            for t in range(SUB):
                last = nc.vector.tensor_scalar(mask_b[:, t, :], adj_i[:, :], 0, MASKED, ALU.is_le, ALU.mult)
            last.then_inc(mask_ok, 1)
            dve.wait_ge(c_bg, 16)

            def step(t, groups, q, m):
                g1, g2, g3, g4, _ = groups
                normed = g1 is not None or g3 is not None
                if g1 is not None:
                    dve.wait_ge(x_in[q], 16 * (m + 1))
                if g2 is not None:
                    dve.wait_ge(z_ok, g2 + 1)
                    nc.vector.scalar_tensor_tensor(score[:, :, :], z[:, :, :], SLOPE, z[:, :, :], ALU.mult, ALU.max
                                                   ).then_inc(score_ok, 1)
                if normed:
                    for j in range(SUB):
                        if g1 is not None:
                            last = nc.vector.bn_stats(bn[:, 0, j, :], x_all[:, bass.ds(g1, 1), j, :].rearrange("p g d -> p (g d)"))
                    for j in range(SUB):
                        if g3 is not None:
                            if j == 0:
                                dve.wait_ge(x2_ok, g3 + 1)
                            last = nc.vector.bn_stats(bn[:, 1, j, :], x2[q][:, j, :])
                    last.then_inc(stats_ok, 1)
                if g2 is not None:
                    dve.wait_ge(score_ok, g2 + 1)
                    nc.vector.tensor_reduce(smax[:, :], score[:, :, :], AX, ALU.max).then_inc(max_ok, 1)
                if normed:
                    dve.wait_ge(stats_ok, t + 1)
                if g4 is not None:
                    dve.wait_ge(logit_ok, g4 + 1)
                if g2 is not None:
                    dve.wait_ge(max_ok, g2 + 1)
                    nc.vector.tensor_scalar(neg_max[:, :], smax[:, :], -1.0, None, ALU.mult).then_inc(neg_ok, 1)
                if normed:
                    for k, g in ((0, g1), (1, g3)):
                        if g is not None:
                            for j in range(SUB):
                                last = nc.vector.bn_aggr(mv[:, k, j, :], bn[:, k, j, :])
                    last.then_inc(aggr_ok, 1)
                if g4 is not None:
                    for j in range(SUB):
                        last = nc.vector.max(top[:, j, :], logit[:, j, :])
                    last.then_inc(top_ok, 1)
                if normed:
                    dve.wait_ge(aggr_ok, t + 1)
                    nc.vector.tensor_scalar(var_eps[:, :], mv[:, :, :, 1].rearrange("p k j -> p (k j)"), EPS, None, ALU.add
                                            ).then_inc(var_ok, 1)
                if g4 is not None:
                    dve.wait_ge(top_ok, g4 + 1)
                    nc.vector.tensor_tensor(gap[:, :], top[:, :, 1], top[:, :, 0], ALU.subtract).then_inc(gap_ok, 1)
                    for j in range(SUB):
                        last = nc.vector.max_index(top_i[:, j, :], top[:, j, :], logit[:, j, :])
                    last.then_inc(topi_ok, 1)
                    if later(m + (q - 2)):
                        dve.wait_ge(rows_out[1 - q], 16 * 2 * SUB * (m + (q - 2)))
                    nc.vector.tensor_copy(rows[1 - q][:, :, ID].bitcast(I32), token_f[:, :]).then_inc(rowid_ok, 1)
                    dve.wait_ge(topi_ok, g4 + 1)
                    nc.vector.tensor_copy(top_f[:, :, :], top_i[:, :, 0:2].rearrange("p t k -> p k t")).then_inc(topf_ok, 1)
                    dve.wait_ge(rowid_ok, g4 + 1)
                    nc.vector.tensor_scalar(token_f[:, :], token_f[:, :], float(GROUP), None, ALU.add).then_inc(token_ok, 1)
                    dve.wait_ge(topf_ok, g4 + 1)
                    nc.vector.tensor_tensor(chosen[:, :, :, :], expert_no,
                                            top_f[:, :, :, None].to_broadcast([P, 2, SUB, E]), ALU.is_equal
                                            ).then_inc(chosen_ok, 1)
                    if later(g4):
                        dve.wait_ge(seen_ok, 5 * g4)
                    nc.vector.tensor_copy(seen_b[:, 0, :], seen_b[:, SUB, :]).then_inc(seen_ok, 1)
                    dve.wait_ge(chosen_ok, g4 + 1)
                    nc.vector.tensor_tensor(chosen_b[:, :, :], chosen[:, 0, :, :], chosen[:, 1, :, :], ALU.add
                                            ).then_inc(chosenb_ok, 1)
                if g1 is not None:
                    dve.wait_ge(rstd_ok, t + 1)
                    if later(g1):
                        dve.wait_ge(xn1_ps, g1)
                    for j in range(SUB):
                        last = nc.vector.tensor_scalar(xn1[:, j, :], x_all[:, bass.ds(g1, 1), j, :].rearrange("p g d -> p (g d)"),
                                                       mv[:, 0, j, 0:1], rstd[:, j:j + 1], ALU.subtract, ALU.mult)
                    last.then_inc(xn1_ok, 1)
                if g3 is not None:
                    dve.wait_ge(rstd_ok, t + 1)
                    if later(g3):
                        dve.wait_ge(rowx_ok, g3)
                    for j in range(SUB):
                        last = nc.vector.tensor_scalar(xn2[:, j, :], x2[q][:, j, :], mv[:, 1, j, 0:1],
                                                       rstd[:, SUB + j:SUB + j + 1], ALU.subtract, ALU.mult)
                    last.then_inc(xn2_ok, 1)
                if g4 is not None:
                    for j in range(SUB):
                        if j == 0:
                            dve.wait_ge(chosenb_ok, g4 + 1)
                        dve.wait_ge(seen_ok, 5 * g4 + (1 + j))
                        nc.vector.tensor_tensor(seen_b[:, j + 1, :], seen_b[:, j, :], chosen_b[:, j, :], ALU.add
                                                ).then_inc(seen_ok, 1)
                        if j == 0:
                            dve.wait_ge(gape_ok, g4 + 1)
                            nc.vector.tensor_scalar(gap_1[:, :], gap_e[:, :], 1.0, None, ALU.add).then_inc(gap1_ok, 1)
                        if j == 1:
                            dve.wait_ge(gap1_ok, g4 + 1)
                            nc.vector.reciprocal(gate_p[:, 0, :], gap_1[:, :]).then_inc(p1_ok, 1)
                        if j == 2:
                            dve.wait_ge(p1_ok, g4 + 1)
                            nc.vector.tensor_tensor(gate_p[:, 1, :], gap_e[:, :], gate_p[:, 0, :], ALU.mult).then_inc(p2_ok, 1)
                if g2 is not None:
                    dve.wait_ge(exp_ok, g2 + 1)
                    nc.vector.reciprocal(inv_sum[:, :], psum_row[:, :]).then_inc(inv_ok, 1)
                if g4 is not None:
                    dve.wait_ge(p2_ok, g4 + 1)
                    nc.vector.tensor_tensor(weighed[:, :, :, :], chosen[:, :, :, :],
                                            gate_p[:, :, :, None].to_broadcast([P, 2, SUB, E]), ALU.mult
                                            ).then_inc(weighed_ok, 1)
                if g2 is not None:
                    dve.wait_ge(inv_ok, g2 + 1)
                    dve.wait_ge(av_ps, g2 + 1)
                    nc.vector.tensor_tensor(hn[:, :, :], ps_av[:, :].rearrange("p (t d) -> p t d", t=SUB),
                                            inv_sum[:, :, None].to_broadcast([P, SUB, D]), ALU.mult).then_inc(hn_ok, 1)
                if g4 is not None:
                    dve.wait_ge(rank_ps, g4 + 1)
                    nc.vector.tensor_tensor(rank[:, :, :], ps_rank.rearrange("p (t e) -> p t e", t=SUB),
                                            cst[:, C_BASE:C_TOKEN].rearrange("p (t e) -> p t e", t=SUB), ALU.add
                                            ).then_inc(rank_ok, 1)
                if g2 is not None:
                    dve.wait_ge(hn_ok, g2 + 1)
                    nc.vector.tensor_scalar(hmin[:, :, :], hn[:, :, :], 0.0, None, ALU.min).then_inc(min_ok, 1)
                if g4 is not None:
                    dve.wait_ge(rank_ok, g4 + 1)
                    nc.vector.tensor_tensor(slot_p[:, :, :, :], chosen[:, :, :, :],
                                            rank[:, None, :, :].to_broadcast([P, 2, SUB, E]), ALU.mult
                                            ).then_inc(slotp_ok, 1)
                    dve.wait_ge(weighed_ok, g4 + 1)
                    nc.vector.tensor_tensor(rows[1 - q][:, :, D:ID], weighed[:, 0, :, :], weighed[:, 1, :, :], ALU.add
                                            ).then_inc(rowp_ok, 1)
                    dve.wait_ge(slotp_ok, g4 + 1)
                    with nc.allow_low_precision(reason="one term of a sum is a slot's number, the others are zero"):
                        nc.vector.tensor_reduce(slot_i[1 - q][:, :], slot_p[:, :, :, :].rearrange("p k t e -> p (k t) e"),
                                                AX, ALU.add).then_inc(slot_ok, 1)
                if g2 is not None:
                    dve.wait_ge(hexp_ok, g2 + 1)
                    nc.vector.scalar_tensor_tensor(helu[:, :, :], hexp[:, :, :], -1.0, hn[:, :, :], ALU.add, ALU.max
                                                   ).then_inc(helu_ok, 1)
                if g3 is not None:
                    dve.wait_ge(gate_ps, g3 + 1)
                    nc.vector.tensor_tensor(logit[:, :, :], ps_gate.rearrange("p (t e) -> p t e", t=SUB),
                                            bg_sb[:, None, :].to_broadcast([P, SUB, E]), ALU.add).then_inc(logit_ok, 1)
                if g2 is not None:
                    dve.wait_ge(helu_ok, g2 + 1)
                    if later(m + (q - 1)):
                        dve.wait_ge(stored[1 - q], 16 * (m + (q - 1)))
                    nc.vector.tensor_tensor(x2[1 - q][:, :, :], helu[:, :, :],
                                            x_all[:, bass.ds(g2, 1), :, :].rearrange("p g s d -> p (g s) d"), ALU.add
                                            ).then_inc(x2_ok, 1)

            by_steps(dve, step)

            dve.wait_ge(count_ps, 1)
            nc.vector.tensor_copy(count_f[:, :], ps_count).then_inc(count_ok, 1)
            dve.wait_ge(count_ok, 1)
            nc.vector.tensor_copy(count_i[:, :], count_f[:, :])
            nc.vector.tensor_scalar(blocks_f[:, :], count_f[:, :], float(GROUP - 1), 1.0 / GROUP, ALU.add, ALU.mult
                                    ).then_inc(blocks_ok, 1)
            dve.wait_ge(blocks_ok, 1)
            nc.vector.tensor_scalar(blocks_i[:, :], blocks_f[:, :], 0.5 - 0.5 / GROUP, None, ALU.subtract).then_inc(blocks_ok, 1)
            dve.wait_ge(blocks_ok, 2)
            nc.vector.tensor_copy(blocks_r[:, :], blocks_i[:, :]).then_inc(blocks_ok, 1)
            dve.wait_ge(blocks_ok, 3)
            nc.vector.tensor_scalar(blocks_m[:, :], blocks_r[:, :], 1.0, None, ALU.max).then_inc(blocks_ok, 1)
            dve.wait_ge(blocks_ok, 4)
            nc.vector.tensor_tensor_scan(until_f[:, :], ones8[:, :], blocks_m[:, :], 0.0, ALU.mult, ALU.add).then_inc(blocks_ok, 1)
            dve.wait_ge(blocks_ok, 5)
            nc.vector.tensor_copy(until_i[:, :], until_f[:, :]).then_inc(table_ok, 1)
            bounds = block_bounds(dve)

            def rest_x(i):
                dve.wait_ge(xh_ok, i + 1)
                nc.vector.tensor_tensor(xl[:, :], ps_x[:, :], xh[:, :].bitcast(F32), ALU.subtract).then_inc(xl_ok, 1)
                dve.wait_ge(own_ok, i + FIRST)
                nc.vector.tensor_copy(meta[:, :, :], xs[:, :, D:ROW]).then_inc(meta_ok, 1)

            def weigh(i):
                parity = (i + 2) & 1
                dve.wait_ge(yt_ps, i + 2)
                for pair in range(2):
                    for t in (2 * pair, 2 * pair + 1):
                        dve.wait_ge(added[t], 16 * (i + 1))
                        nc.vector.tensor_scalar(ys[t][:, :], ps_yt[:, t * D:(t + 1) * D],
                                                wgt[:, bass.ds(parity, 1), t], None, ALU.mult)
                        last = nc.vector.tensor_copy(ysi[t][:, :], tid[:, bass.ds(parity, 1), t])
                    last.then_inc(ys_ok, 1)

            rest_x(0)
            for e in range(E):
                with dve.Fori(bounds[e], bounds[e + 1]) as i:
                    dve.wait_ge(meta_ok, i + FIRST + 1)
                    dve.wait_ge(ys_ok, 2 * i + FIRST)
                    nc.vector.tensor_copy(wgt[:, bass.ds(i & 1, 1), :], meta[:, :, e:e + 1].rearrange("p t k -> p k t"))
                    nc.vector.tensor_copy(tid[:, bass.ds(i & 1, 1), :],
                                          meta[:, :, E:E + 1].rearrange("p t k -> p k t").bitcast(I32)).then_inc(own_ok, 1)
                    for c in range(HC):
                        dve.wait_ge(r_ok, HC * i + (c + 1))
                        nc.vector.tensor_copy(hh[:, c, :], hr[:, c, :]).then_inc(hh_ok, 1)
                        if c:
                            dve.wait_ge(hh_ok, HC * i + c)
                            nc.vector.tensor_tensor(hl[:, c - 1, :], hr[:, c - 1, :], hh[:, c - 1, :].bitcast(F32), ALU.subtract
                                                    ).then_inc(hl_ok, 1)
                    dve.wait_ge(hh_ok, HC * i + HC)
                    nc.vector.tensor_tensor(hl[:, HC - 1, :], hr[:, HC - 1, :], hh[:, HC - 1, :].bitcast(F32), ALU.subtract
                                            ).then_inc(hl_ok, 1)
                    rest_x(i + 1)
                    weigh(i - 1)
            dve.wait_ge(own_ok, bounds[E] + FIRST)
            weigh(bounds[E] - 1)

        @block.tensor
        def _(pe):
            pe.wait_ge(c_cst, 16)
            pe.wait_ge(c_wt, 16)
            pe.wait_ge(a_rep_ok, 1)
            nc.tensor.matmul(ps_setup[:, 0:P], wt_sb[:, :], a_rep[:, 0, :], start=True, stop=True).then_inc(xs_ps, FIRST)
            nc.tensor.matmul(ps_setup[:, P:2 * P], wt_sb[:, :], a_rep[:, 1, :], start=True, stop=True).then_inc(wa_ps, 1)
            pe.wait_ge(wa_ok, 1)
            pe.wait_ge(mask_ok, 1)
            pe.wait_ge(c_w, 16)
            pe.wait_ge(c_wg, 16)

            def tiles(ap):
                return ap[:, :].rearrange("p (t j) -> p t j", t=SUB)

            def step(t, groups, q, m):
                g1, g2, g3, g4, _ = groups
                if g2 is not None:
                    pe.wait_ge(exp_ok, g2 + 1)
                    if later(g2):
                        pe.wait_ge(prob_t_ok, g2)
                    for j in range(SUB):
                        last = nc.tensor.transpose(tiles(ps_tp)[:, j, :], prob[:, j, :], ident)
                    last.then_inc(prob_ps, 1)
                if g1 is not None:
                    pe.wait_ge(xn1_ok, g1 + 1)
                    if later(g1):
                        pe.wait_ge(xn1_t_ok, g1)
                    for j in range(SUB):
                        last = nc.tensor.transpose(tiles(ps_t1)[:, j, :], xn1[:, j, :], ident)
                    last.then_inc(xn1_ps, 1)
                if g2 is not None:
                    pe.wait_ge(prob_t_ok, g2 + 1)
                    pe.wait_ge(wh_ok, g2 + 1)
                    if later(g2):
                        pe.wait_ge(hn_ok, g2)
                    for j in range(SUB):
                        last = nc.tensor.matmul(tiles(ps_av)[:, j, :], prob_t[:, j, :], wh[1 - q][:, j, :], start=True, stop=True)
                    last.then_inc(av_ps, 1)
                if g3 is not None:
                    pe.wait_ge(xn2_ok, g3 + 1)
                    if later(g3):
                        pe.wait_ge(xn2_t_ok, g3)
                    for j in range(SUB):
                        last = nc.tensor.transpose(tiles(ps_t3)[:, j, :], xn2[:, j, :], ident)
                    last.then_inc(xn2_ps, 1)
                if g4 is not None:
                    pe.wait_ge(seen_ok, 5 * g4 + 5)
                    if later(g4):
                        pe.wait_ge(rank_ok, g4)
                    nc.tensor.matmul(ps_rank, before_b[:, :], chosen_b[:, :, :], start=True, stop=False)
                    nc.tensor.matmul(ps_rank, ones_b[:, :], seen_b[:, 0:SUB, :], start=False, stop=True).then_inc(rank_ps, 1)
                if g1 is not None:
                    pe.wait_ge(xn1_t_ok, g1 + 1)
                    if later(g1):
                        pe.wait_ge(z_ok, g1)
                    nc.tensor.matmul(ps_z[:, :], ident_b[:, :], mask_b[:, :, :], start=True, stop=False)
                    nc.tensor.matmul(ps_z[:, :], w_a[:, 1, :], xn1_t[:, :], start=False, stop=False)
                    for j in range(SUB):
                        last = nc.tensor.matmul(tiles(ps_z)[:, j, :], xn1_t[:, j * P:(j + 1) * P], w_a[:, 0, :],
                                                start=False, stop=j == SUB - 1)
                    last.then_inc(z_ps, 1)
                if g3 is not None:
                    pe.wait_ge(xn2_t_ok, g3 + 1)
                    if later(g3):
                        pe.wait_ge(logit_ok, g3)
                    for j in range(SUB):
                        last = nc.tensor.matmul(ps_gate[:, j * E:(j + 1) * E], xn2_t[:, j * P:(j + 1) * P], wg_sb[:, :],
                                                start=True, stop=True)
                    last.then_inc(gate_ps, 1)
                if g1 is not None:
                    if later(g1):
                        pe.wait_ge(wh_ok, g1)
                    for j in range(SUB):
                        last = nc.tensor.matmul(tiles(ps_wh)[:, j, :], xn1_t[:, j * P:(j + 1) * P], w_sb[:, :],
                                                start=True, stop=True)
                    last.then_inc(wh_ps, 1)

            by_steps(pe, step)
            pe.wait_ge(rank_ok, GROUPS)
            nc.tensor.matmul(ps_count, ones_b[:, :], seen_b[:, SUB, :], start=True, stop=True).then_inc(count_ps, 1)
            bounds = block_bounds(pe)
            pe.wait_ge(lo_ok, 4)

            def transpose_x(i):
                pe.wait_ge(xs_in, 16 * (i + 1))
                for t in range(SUB):
                    last = nc.tensor.transpose(ps_x[:, t * P:(t + 1) * P], xs[:, t, 0:D], ident)
                last.then_inc(xs_ps, 1)

            def transpose_y(i):
                pe.wait_ge(yb_ok, i + (FIRST + 1))
                pe.wait_ge(ys_ok, 2 * i + (2 + FIRST))
                for t in range(SUB):
                    last = nc.tensor.transpose(ps_yt[:, t * D:(t + 1) * D], yb[:, t * P:(t + 1) * P], ident)
                last.then_inc(yt_ps, 1)

            transpose_x(0)
            for e in range(E):
                with pe.Fori(bounds[e], bounds[e + 1]) as i:
                    pe.wait_ge(xl_ok, i + 1)
                    for c in range(HC):
                        chunk = slice(c * P, (c + 1) * P)
                        nc.tensor.matmul(ps_h[c][:, :], w1_hi[:, e, chunk], xh[:, :], start=True, stop=False)
                        nc.tensor.matmul(ps_h[c][:, :], w1_hi[:, e, chunk], xl[:, :], start=False, stop=False)
                        nc.tensor.matmul(ps_h[c][:, :], w1_lo[:, e, chunk], xh[:, :], start=False, stop=True
                                         ).then_inc(h_ps, 1)
                    transpose_x(i + 1)
                    transpose_y(i - 1)
                    for c in range(HC):
                        pe.wait_ge(hl_ok, HC * i + (c + 1))
                        nc.tensor.matmul(ps_y[:, :], w2_hi[:, e, c, :], hh[:, c, :], start=c == 0, stop=False)
                        nc.tensor.matmul(ps_y[:, :], w2_hi[:, e, c, :], hl[:, c, :], start=False, stop=False)
                        last = nc.tensor.matmul(ps_y[:, :], w2_lo[:, e, c, :], hh[:, c, :], start=False, stop=c == HC - 1)
                    last.then_inc(y_ps, 1)
            transpose_y(bounds[E] - 1)


def kernel(x, adj, L0_gnn_W, L0_gnn_a, L0_ffn_Wg, L0_ffn_bg, L0_ffn_W1, L0_ffn_b1, L0_ffn_W2, L0_ffn_b2):
    import numpy as np
    import concourse.bacc as bacc
    from concourse.bass_utils import run_bass_kernel_spmd

    def laid(v):
        return np.ascontiguousarray(v)

    w1, w2 = np.asarray(L0_ffn_W1), np.asarray(L0_ffn_W2)
    arrays = {
        "x": laid(np.asarray(x).reshape(TOKENS, D)),
        "adj": laid(np.asarray(adj)),
        "w": laid(np.asarray(L0_gnn_W)),
        "wt": laid(np.asarray(L0_gnn_W).T),
        "a": laid(np.asarray(L0_gnn_a).reshape(2, D).T),
        "wg_t": laid(np.asarray(L0_ffn_Wg).T),
        "bg": laid(np.asarray(L0_ffn_bg)),
        "w1_t": laid(w1.transpose(2, 0, 1)),
        "b1_t": laid(np.asarray(L0_ffn_b1).reshape(E, HC, P).transpose(2, 0, 1)),
        "w2_t": laid(w2.reshape(E, D, HC, P).transpose(3, 0, 2, 1)),
        "b2_t": laid(np.asarray(L0_ffn_b2).T),
        "consts": shape_constants(np),
    }
    nc = bacc.Bacc("TRN2", target_bir_lowering=False, num_devices=1)
    aps = {n: nc.dram_tensor(n, v.shape, mybir.dt.from_np(v.dtype), kind="ExternalInput").ap() for n, v in arrays.items()}
    out = nc.dram_tensor("out", (TOKENS + GROUP, D), F32, kind="ExternalOutput").ap()
    gnn_moe_kernel(nc, **aps, out=out)
    r = run_bass_kernel_spmd(nc, [arrays], core_ids=[0])
    return r.results[0]["out"][:TOKENS].reshape(128, NODES, D)
```

```python
import concourse.bass as bass
from concourse import mybir
from contextlib import ExitStack

F32 = mybir.dt.float32
F32R = mybir.dt.float32r
BF16 = mybir.dt.bfloat16
I32 = mybir.dt.int32
U32 = mybir.dt.uint32
ALU = mybir.AluOpType
ACT = mybir.ActivationFunctionType
AX = mybir.AxisListType.X

P = 128
NODES = 64
TOKENS = 128 * NODES
D = 128
H = 512
E = 8
SUB = 4
GROUP = SUB * P
GROUPS = TOKENS // GROUP
HC = H // P
ROW = D + E + 1
ID = D + E
CAP = TOKENS + GROUP
EPS = 1e-5
SLOPE = 0.2
STAGES = 5
MASKED = -1e30
FIRST = 1

C_IDENT = 0
C_BEFORE = C_IDENT + P
C_EXPERT = C_BEFORE + P
C_BASE = C_EXPERT + 2 * SUB * E
C_TOKEN = C_BASE + SUB * E
C_PAD = C_TOKEN + SUB
C_END = C_PAD + SUB


def shape_constants(np):
    c = np.zeros((P, C_END), np.float32)
    c[:, C_IDENT:C_IDENT + P] = np.eye(P)
    c[:, C_BEFORE:C_BEFORE + P] = np.triu(np.ones((P, P)), 1)
    c[:, C_EXPERT:C_BASE] = np.tile(np.arange(E), 2 * SUB)
    c[:, C_BASE:C_TOKEN] = np.tile(np.arange(E) * CAP, SUB)
    c[:, C_TOKEN:C_PAD] = np.arange(SUB)[None, :] * P + np.arange(P)[:, None] - GROUP
    c[:, C_PAD:C_END] = TOKENS + np.arange(P)[:, None] * SUB + np.arange(SUB)[None, :]
    return c


def gnn_moe_kernel(nc, x, adj, w, wt, a, wg_t, bg, w1_t, b1_t, w2_t, b2_t, consts, out):
    ctx = ExitStack()
    with ctx:
        def sb(name, shape, dt=F32):
            return ctx.enter_context(nc.sbuf_tensor(name, shape, dt))

        def sem(name):
            return ctx.enter_context(nc.semaphore(name))

        slots = nc.dram_tensor("expert_slots", [E * CAP, ROW], F32, kind="Internal").ap()
        x_groups = x.rearrange("(g s p) d -> g p s d", s=SUB, p=P)
        out_groups = out[0:TOKENS, :].rearrange("(g s p) d -> g p s d", s=SUB, p=P)

        cst = sb("cst", [P, C_END])
        ident = cst[:, C_IDENT:C_IDENT + P]
        expert_no = cst[:, C_EXPERT:C_BASE].rearrange("p (k s e) -> p k s e", k=2, s=SUB)
        ident_b = sb("ident_b", [P, P], BF16)
        before_b = sb("before_b", [P, P], BF16)
        ones_b = sb("ones_b", [P, P], BF16)
        minus_half = sb("minus_half", [P, 2 * SUB])
        act_scratch = sb("act_scratch", [P, 1])
        pool_scratch = sb("pool_scratch", [P, 1])
        w_sb = sb("w_sb", [P, D])
        wt_sb = sb("wt_sb", [P, D])
        a_sb = sb("a_sb", [P, 2])
        a_rep = sb("a_rep", [P, 2, P])
        w_a = sb("w_a", [P, 2, P])
        adj_i = sb("adj_i", [P, P], I32)
        mask_b = sb("mask_b", [P, SUB, P], BF16)
        wg_sb = sb("wg_sb", [P, E])
        bg_sb = sb("bg_sb", [P, E])
        b1_sb = sb("b1_sb", [P, E, HC])
        b2_sb = sb("b2_sb", [P, E])
        w1_raw = sb("w1_raw", [P, E, H])
        w2_raw = sb("w2_raw", [P, E, HC, D])
        w1_hi = sb("w1_hi", [P, E, H], F32R)
        w1_lo = sb("w1_lo", [P, E, H], F32R)
        w2_hi = sb("w2_hi", [P, E, HC, D], F32R)
        w2_lo = sb("w2_lo", [P, E, HC, D], F32R)
        pad_rows = sb("pad_rows", [P, SUB, ROW])

        x_all = sb("x_all", [P, GROUPS, SUB, D])
        bn = sb("bn", [P, 2, SUB, 6])
        mv = sb("mv", [P, 2, SUB, 2])
        var_eps = sb("var_eps", [P, 2 * SUB])
        rstd = sb("rstd", [P, 2 * SUB])
        shift = sb("shift", [P, SUB])
        xn1 = sb("xn1", [P, SUB, D])
        xn1_t = sb("xn1_t", [P, GROUP])
        z = sb("z", [P, SUB, P])
        wh = sb("wh", [P, SUB, D])
        score = sb("score", [P, SUB, P])
        smax = sb("smax", [P, SUB])
        neg_max = sb("neg_max", [P, SUB])
        prob = sb("prob", [P, SUB, P])
        psum_row = sb("psum_row", [P, SUB])
        prob_t = sb("prob_t", [P, SUB, P])
        inv_sum = sb("inv_sum", [P, SUB])
        hrelu = sb("hrelu", [P, SUB, D])
        hexp = sb("hexp", [P, SUB, D])
        u = sb("u", [P, SUB, D])
        xr = sb("xr", [P, SUB, D])
        x2 = [sb(f"x2_{q}", [P, SUB, D]) for q in range(2)]
        xn2 = [sb(f"xn2_{q}", [P, SUB, D]) for q in range(2)]
        rows = [sb(f"rows{q}", [P, SUB, ROW]) for q in range(2)]
        xn2_t = sb("xn2_t", [P, GROUP])
        logit = sb("logit", [P, SUB, E])
        top = sb("top", [P, SUB, 8])
        top_i = sb("top_i", [P, SUB, 8], U32)
        gap = sb("gap", [P, SUB])
        gap_e = sb("gap_e", [P, SUB])
        gap_1 = sb("gap_1", [P, SUB])
        top_f = sb("top_f", [P, 2, SUB])
        gate_p = sb("gate_p", [P, 2, SUB])
        chosen = sb("chosen", [P, 2, SUB, E])
        weighed = sb("weighed", [P, 2, SUB, E])
        chosen_b = sb("chosen_b", [P, SUB, E], BF16)
        seen_b = sb("seen_b", [P, SUB + 1, E], BF16)
        rank = sb("rank", [P, SUB, E])
        slot_p = sb("slot_p", [P, 2, SUB, E])
        slot_i = [sb(f"slot_i{q}", [P, 2 * SUB], I32) for q in range(2)]
        token_f = sb("token_f", [P, SUB])
        count_f = sb("count_f", [P, E])
        count_i = sb("count_i", [P, E], I32)
        blocks_f = sb("blocks_f", [P, E])
        blocks_i = sb("blocks_i", [P, E], I32)
        blocks_r = sb("blocks_r", [P, E])
        blocks_m = sb("blocks_m", [P, E])
        ones8 = sb("ones8", [P, E])
        until_f = sb("until_f", [P, E])
        until_i = sb("until_i", [P, E], I32)

        xs = sb("xs", [P, SUB, ROW])
        xh = sb("xh", [P, GROUP], F32R)
        xl = sb("xl", [P, GROUP], F32R)
        meta = sb("meta", [P, SUB, E + 1])
        wgt = sb("wgt", [P, 2, SUB])
        tid = sb("tid", [P, 2, SUB], I32)
        hr = x_all[:, 0:HC, :, :].rearrange("p c s d -> p c (s d)")
        hh = sb("hh", [P, HC, GROUP], F32R)
        hl = sb("hl", [P, HC, GROUP], F32R)
        yb = sb("yb", [P, GROUP])
        ys = [sb(f"ys{s}", [P, D]) for s in range(SUB)]
        ysi = [sb(f"ysi{s}", [P, 1], I32) for s in range(SUB)]

        bank = [ctx.enter_context(nc.psum_tensor(f"bank{n}", [P, 512], F32)) for n in range(8)]
        ps_t1, ps_z, ps_wh, ps_tp, ps_av, ps_t3, ps_route, ps_setup = bank
        ps_gate, ps_rank, ps_count = ps_route[:, 0:SUB * E], ps_setup[:, 0:SUB * E], ps_setup[:, 64:64 + E]
        ps_h = bank[0:4]
        ps_x, ps_y, ps_yt = bank[4:7]

        c_w = sem("c_w")
        c_wt = sem("c_wt")
        c_a = sem("c_a")
        c_adj0 = sem("c_adj0")
        c_adj1 = sem("c_adj1")
        c_cst = sem("c_cst")
        c_wg = sem("c_wg")
        c_bg = sem("c_bg")
        c_b1 = sem("c_b1")
        c_b2 = sem("c_b2")
        c_w1 = sem("c_w1")
        c_w2 = sem("c_w2")
        int_zeros = sem("int_zeros")
        row_zeros = sem("row_zeros")
        start_ok = sem("start_ok")
        a_rep_ok = sem("a_rep_ok")
        wa_ps = sem("wa_ps")
        wa_ok = sem("wa_ok")
        mask_ok = sem("mask_ok")
        pads_ok = sem("pads_ok")
        hi_ok = sem("hi_ok")
        lo_ok = sem("lo_ok")
        stats1_ok = sem("stats1_ok")
        stats2_ok = sem("stats2_ok")
        aggr1_ok = sem("aggr1_ok")
        aggr2_ok = sem("aggr2_ok")
        var_ok = sem("var_ok")
        rstd_ok = sem("rstd_ok")
        shift_ok = sem("shift_ok")
        xn1_ok = sem("xn1_ok")
        xn1_ps = sem("xn1_ps")
        xn1_t_ok = sem("xn1_t_ok")
        z_ps = sem("z_ps")
        wh_ps = sem("wh_ps")
        z_ok = sem("z_ok")
        wh_ok = sem("wh_ok")
        score_ok = sem("score_ok")
        max_ok = sem("max_ok")
        neg_ok = sem("neg_ok")
        exp_ok = sem("exp_ok")
        prob_ps = sem("prob_ps")
        prob_t_ok = sem("prob_t_ok")
        av_ps = sem("av_ps")
        inv_ok = sem("inv_ok")
        hrelu_ok = sem("hrelu_ok")
        hexp_ok = sem("hexp_ok")
        xr_ok = sem("xr_ok")
        u_ok = sem("u_ok")
        x2_ok = sem("x2_ok")
        xn2_ok = sem("xn2_ok")
        xn2_ps = sem("xn2_ps")
        xn2_t_ok = sem("xn2_t_ok")
        gate_ps = sem("gate_ps")
        logit_ok = sem("logit_ok")
        top_ok = sem("top_ok")
        topi_ok = sem("topi_ok")
        gap_ok = sem("gap_ok")
        gape_ok = sem("gape_ok")
        gap1_ok = sem("gap1_ok")
        topf_ok = sem("topf_ok")
        p1_ok = sem("p1_ok")
        p2_ok = sem("p2_ok")
        chosen_ok = sem("chosen_ok")
        weighed_ok = sem("weighed_ok")
        chosenb_ok = sem("chosenb_ok")
        rowid_ok = sem("rowid_ok")
        rowx_ok = sem("rowx_ok")
        rowp_ok = sem("rowp_ok")
        seen_ok = sem("seen_ok")
        rank_ps = sem("rank_ps")
        rank_ok = sem("rank_ok")
        slotp_ok = sem("slotp_ok")
        token_ok = sem("token_ok")
        slot_ok = sem("slot_ok")
        count_ps = sem("count_ps")
        count_ok = sem("count_ok")
        blocks_ok = sem("blocks_ok")
        table_ok = sem("table_ok")
        pads_out = sem("pads_out")
        xs_in = sem("xs_in")
        xs_ps = sem("xs_ps")
        xh_ok = sem("xh_ok")
        xl_ok = sem("xl_ok")
        meta_ok = sem("meta_ok")
        own_ok = sem("own_ok")
        h_ps = sem("h_ps")
        r_ok = sem("r_ok")
        hh_even_ok = sem("hh_even_ok")
        hh_odd_ok = sem("hh_odd_ok")
        hl_ok = sem("hl_ok")
        y_ps = sem("y_ps")
        yb_ok = sem("yb_ok")
        yt_ps = sem("yt_ps")
        ys_ok = sem("ys_ok")
        dump_ok = sem("dump_ok")
        stood = sem("stood")
        x_in, rows_out, stored = ([sem(f"{n}{q}") for q in range(2)] for n in ("x_in", "rows_out", "stored"))
        added = [sem(f"added{t}") for t in range(SUB)]

        def tiles(ap):
            return ap[:, :].rearrange("p (t j) -> p t j", t=SUB)

        def later(n):
            return not isinstance(n, int) or n > 0

        def by_steps(eng, step):
            def at(t):
                step(t, [t - n if 0 <= t - n < GROUPS else None for n in range(STAGES)], t % 2, t // 2)

            for t in range(6):
                at(t)
            with eng.Fori(3, GROUPS // 2) as m:
                for q in range(2):
                    step(2 * m + q, [2 * m + (q - n) for n in range(STAGES)], q, m)
            for t in range(GROUPS, GROUPS + STAGES - 1):
                at(t)

        def block_bounds(eng):
            eng.wait_ge(table_ok, 1)
            return [0] + [eng.value_load(until_i[0:1, e:e + 1], min_val=1, max_val=TOKENS * 2 // GROUP + E)
                          for e in range(E)]

        block = ctx.enter_context(nc.Block())

        @block.sync
        def _(sp):
            sp.dma_start(a_sb[:, :], a).then_inc(c_a, 16)
            sp.dma_start(cst[:, :], consts).then_inc(c_cst, 16)
            sp.dma_start(x_all[:, 0, :, :], x_groups[0]).then_inc(x_in[0], 16)
            sp.dma_start(wt_sb[:, :], wt).then_inc(c_wt, 16)
            sp.wait_ge(int_zeros, 1)
            sp.dma_start(adj_i[0:NODES, 0:NODES], adj).then_inc(c_adj0, 16)
            sp.dma_start(adj_i[NODES:P, NODES:P], adj).then_inc(c_adj1, 16)
            sp.dma_start(w_sb[:, :], w).then_inc(c_w, 16)
            sp.dma_start(x_all[:, 1, :, :], x_groups[1]).then_inc(x_in[1], 16)
            sp.dma_start(wg_sb[:, :], wg_t).then_inc(c_wg, 16)
            sp.dma_start(bg_sb[:, :], bg.partition_broadcast(P)).then_inc(c_bg, 16)
            with sp.Fori(1, GROUPS // 2) as m:
                for q in range(2):
                    sp.wait_ge(x_in[q], 16 * m)
                    sp.dma_start(x_all[:, bass.ds(2 * m + q, 1), :, :],
                                 x_groups[bass.ds(2 * m + q, 1)].rearrange("g p s d -> p g s d")).then_inc(x_in[q], 16)
            sp.dma_start(w1_raw[:, :, :], w1_t).then_inc(c_w1, 16)
            sp.dma_start(w2_raw[:, :, :, :], w2_t).then_inc(c_w2, 16)
            sp.dma_start(b1_sb[:, :, :], b1_t).then_inc(c_b1, 16)
            sp.dma_start(b2_sb[:, :], b2_t).then_inc(c_b2, 16)
            sp.wait_ge(pads_ok, 1)
            sp.dma_start(out[TOKENS:TOKENS + GROUP, :].rearrange("(p s) d -> p s d", s=SUB),
                         pad_rows[:, :, 0:D]).then_inc(dump_ok, 16)
            with sp.Fori(0, GROUPS // 2) as m:
                for q in range(2):
                    sp.wait_ge(x2_ok, 2 * m + (q + 1))
                    sp.dma_start(out_groups[bass.ds(2 * m + q, 1)].rearrange("g p s d -> p g s d"),
                                 x2[q][:, :, :].rearrange("p (g s) d -> p g s d", g=1)).then_inc(stored[q], 16)
            sp.wait_ge(table_ok, 1)
            for e in range(E):
                n = sp.value_load(count_i[0:1, e:e + 1], min_val=0, max_val=TOKENS)
                sp.dma_start(slots[bass.ds(n + e * CAP, GROUP), :].rearrange("(p s) r -> p s r", s=SUB),
                             pad_rows[:, :, :]).then_inc(pads_out, 16)
            bounds = block_bounds(sp)
            sp.wait_ge(pads_out, 16 * E)
            for q in range(2):
                sp.wait_ge(rows_out[q], 16 * 2 * SUB * (GROUPS // 2))

            def load_block(first_row, i):
                sp.wait_ge(xs_ps, i + FIRST)
                sp.wait_ge(meta_ok, i + FIRST)
                sp.dma_start(xs[:, :, :], slots[bass.ds(first_row, GROUP), :].rearrange("(p s) r -> p s r", s=SUB)
                             ).then_inc(xs_in, 16)

            for e in range(E):
                with sp.Fori(bounds[e], bounds[e + 1]) as i:
                    row = nc.s_assert_within((i - bounds[e]) * GROUP + e * CAP, e * CAP, (e + 1) * CAP - GROUP,
                                             skip_runtime_bounds_check_because="an expert has at most TOKENS tokens")
                    load_block(row, i)
            load_block(0, bounds[E])
            for q in range(2):
                sp.wait_ge(stored[q], 16 * (GROUPS // 2))

        def stand(pool, before):
            pool.wait_ge(stood, before + FIRST)
            nc.gpsimd.tensor_tensor(pool_scratch[:, :], minus_half[:, 0:1], minus_half[:, 0:1], ALU.add
                                    ).then_inc(stood, 1)

        @block.gpsimd
        def _(pool):
            nc.gpsimd.memset(adj_i[:, :], 0).then_inc(int_zeros, 1)
            nc.gpsimd.memset(minus_half[:, :], -0.5).then_inc(stood, FIRST)
            nc.gpsimd.memset(pad_rows[:, :, :], 0.0).then_inc(row_zeros, 1)
            pool.wait_ge(c_cst, 16)
            pool.wait_ge(row_zeros, 1)
            nc.gpsimd.tensor_copy(pad_rows[:, :, ID].bitcast(I32), cst[:, C_PAD:C_END]).then_inc(pads_ok, 1)

            def step(t, groups, q, m):
                g0, _, gx, _, gr = groups
                if g0 is not None or gx is not None:
                    pool.wait_ge(var_ok, t + 1)
                    if later(t - 2):
                        pool.wait_ge(xn2_ok, SUB * (t - 2))
                    nc.gpsimd.tensor_tensor(rstd[:, :], var_eps[:, :], minus_half[:, :], ALU.pow).then_inc(rstd_ok, 1)
                if gr is not None:
                    pool.wait_ge(slot_ok, gr + 1)
                    pool.wait_ge(rowx_ok, gr + 1)
                    stand(pool, gr)
                    for k in range(2):
                        for j in range(SUB):
                            nc.gpsimd.indirect_dma_start(
                                out=slots, out_offset=bass.IndirectOffsetOnAxis(
                                    ap=slot_i[q][:, k * SUB + j:k * SUB + j + 1], axis=0),
                                in_=rows[q][:, j, :], in_offset=None).then_inc(rows_out[q], 16)

            by_steps(pool, step)
            bounds = block_bounds(pool)
            for q in range(2):
                pool.wait_ge(stored[q], 16 * (GROUPS // 2))
            pool.wait_ge(dump_ok, 16)

            def add_rows(i, experts):
                for t in range(SUB):
                    if t % 2 == 0:
                        pool.wait_ge(ys_ok, 2 * (i + 1) + (FIRST + 1 + t // 2))
                        stand(pool, GROUPS + experts + 2 * (i + 1) + t // 2)
                    nc.gpsimd.indirect_dma_start(
                        out=out, out_offset=bass.IndirectOffsetOnAxis(ap=ysi[t][:, :], axis=0),
                        in_=ys[t][:, :], in_offset=None, compute_op=ALU.add).then_inc(added[t], 16)

            add_rows(-1, 0)
            for e in range(E):
                for t in range(SUB):
                    pool.wait_ge(added[t], bounds[e] * 16 + 16)
                stand(pool, GROUPS + e + 2 * (bounds[e] + 1))
                with pool.Fori(bounds[e], bounds[e + 1]) as i:
                    add_rows(i, e + 1)
            for t in range(SUB):
                pool.wait_ge(added[t], bounds[E] * 16 + 16)

        @block.scalar
        def _(act):
            act.wait_ge(c_cst, 16)
            nc.scalar.copy(act_scratch[:, :], cst[:, 0:1]).then_inc(yb_ok, FIRST)
            act.wait_ge(wa_ps, 1)
            nc.scalar.copy(w_a[:, :, :], ps_setup[:, 0:2 * P].rearrange("p (k j) -> p k j", k=2)).then_inc(wa_ok, 1)

            def step(t, groups, q, m):
                g0, g1, gx, gl, _ = groups
                if g1 is not None:
                    act.wait_ge(neg_ok, g1 + 1)
                    if later(g1):
                        act.wait_ge(prob_ps, g1)
                    for j in range(SUB):
                        nc.scalar.activation(prob[:, j, :], score[:, j, :], ACT.Exp, bias=neg_max[:, j:j + 1],
                                             accum_out=psum_row[:, j:j + 1]).then_inc(exp_ok, 1)
                if gl is not None:
                    act.wait_ge(gap_ok, gl + 1)
                    nc.scalar.activation(gap_e[:, :], gap[:, :], ACT.Exp).then_inc(gape_ok, 1)
                if g1 is not None:
                    act.wait_ge(prob_ps, g1 + 1)
                    if later(g1):
                        act.wait_ge(av_ps, g1)
                    nc.scalar.copy(prob_t[:, :, :], tiles(ps_tp)).then_inc(prob_t_ok, 1)
                if g0 is not None:
                    act.wait_ge(xn1_ps, g0 + 1)
                    if later(g0):
                        act.wait_ge(wh_ps, g0)
                    nc.scalar.copy(xn1_t[:, :], ps_t1[:, :]).then_inc(xn1_t_ok, 1)
                if g1 is not None:
                    act.wait_ge(av_ps, g1 + 1)
                    act.wait_ge(inv_ok, g1 + 1)
                    if later(g1):
                        act.wait_ge(xr_ok, g1)
                        act.wait_ge(u_ok, g1)
                    for j in range(SUB):
                        last = nc.scalar.activation(hrelu[:, j, :], tiles(ps_av)[:, j, :], ACT.Relu, scale=inv_sum[:, j:j + 1])
                    last.then_inc(hrelu_ok, 1)
                    for j in range(SUB):
                        last = nc.scalar.activation(hexp[:, j, :], tiles(ps_av)[:, j, :], ACT.Exp, scale=inv_sum[:, j:j + 1])
                    last.then_inc(hexp_ok, 1)
                if gx is not None:
                    act.wait_ge(shift_ok, gx + 1)
                    if later(gx - 1):
                        act.wait_ge(rowx_ok, gx - 1)
                    for j in range(SUB):
                        nc.scalar.activation(xn2[q][:, j, :], x2[q][:, j, :], ACT.Identity, bias=shift[:, j:j + 1],
                                             scale=rstd[:, SUB + j:SUB + j + 1]).then_inc(xn2_ok, 1)
                if g0 is not None:
                    act.wait_ge(z_ps, g0 + 1)
                    if later(g0):
                        act.wait_ge(score_ok, g0)
                    nc.scalar.copy(z[:, :, :], tiles(ps_z)).then_inc(z_ok, 1)
                if gx is not None:
                    act.wait_ge(xn2_ps, gx + 1)
                    if later(gx):
                        act.wait_ge(gate_ps, gx)
                    nc.scalar.copy(xn2_t[:, :], ps_t3[:, :]).then_inc(xn2_t_ok, 1)
                if g0 is not None:
                    act.wait_ge(wh_ps, g0 + 1)
                    nc.scalar.copy(wh[:, :, :], tiles(ps_wh)).then_inc(wh_ok, 1)
                if gl is not None:
                    if later(m + (q - 2)):
                        act.wait_ge(rows_out[1 - q], 16 * 2 * SUB * (m + (q - 2)))
                    nc.scalar.copy(rows[1 - q][:, :, 0:D], xn2[1 - q][:, :, :]).then_inc(rowx_ok, 1)

            by_steps(act, step)
            act.wait_ge(c_w1, 16)
            act.wait_ge(c_w2, 16)
            for e in range(E):
                nc.scalar.copy(w1_hi[:, e, :], w1_raw[:, e, :])
                nc.scalar.copy(w2_hi[:, e, :, :], w2_raw[:, e, :, :]).then_inc(hi_ok, 1)
            bounds = block_bounds(act)
            act.wait_ge(c_b1, 16)
            act.wait_ge(c_b2, 16)

            def round_x(i):
                act.wait_ge(xs_ps, i + FIRST + 1)
                nc.scalar.copy(xh[:, :], ps_x[:, :]).then_inc(xh_ok, 1)

            round_x(0)
            for e in range(E):
                with act.Fori(bounds[e], bounds[e + 1]) as i:
                    for c in range(HC):
                        act.wait_ge(h_ps, HC * i + (c + 1))
                        nc.scalar.activation(hr[:, c, :], ps_h[c][:, :], ACT.Relu, bias=b1_sb[:, e, c:c + 1]
                                             ).then_inc(r_ok, 1)
                        if c % 2:
                            nc.scalar.activation(hh[:, c, :], ps_h[c][:, :], ACT.Relu, bias=b1_sb[:, e, c:c + 1]
                                                 ).then_inc(hh_odd_ok, 1)
                    round_x(i + 1)
                    act.wait_ge(y_ps, i + 1)
                    nc.scalar.activation(yb[:, :], ps_y[:, :], ACT.Identity, bias=b2_sb[:, e:e + 1]
                                         ).then_inc(yb_ok, 1)

        @block.vector
        def _(dve):
            nc.vector.memset(ones_b[:, :], 1.0)
            nc.vector.memset(ones8[:, :], 1.0).then_inc(meta_ok, FIRST)
            nc.vector.memset(yb[:, :], 0.0).then_inc(ys_ok, FIRST)
            nc.vector.memset(wgt[:, :, :], 0.0).then_inc(own_ok, FIRST)
            nc.vector.memset(mv[:, :, :, :], 1.0)
            nc.vector.memset(seen_b[:, :, :], 0.0).then_inc(start_ok, 1)
            dve.wait_ge(c_cst, 16)
            nc.vector.tensor_copy(ident_b[:, :], ident)
            nc.vector.tensor_copy(before_b[:, :], cst[:, C_BEFORE:C_BEFORE + P])
            nc.vector.tensor_copy(token_f[:, :], cst[:, C_TOKEN:C_PAD])
            for k in range(2):
                nc.vector.tensor_copy(tid[:, k, :], cst[:, C_PAD:C_END])
            dve.wait_ge(start_ok, 1)
            dve.wait_ge(c_a, 16)
            for k in range(2):
                last = nc.vector.tensor_scalar(a_rep[:, k, :], ones_b[:, :], a_sb[:, k:k + 1], None, ALU.mult)
            last.then_inc(a_rep_ok, 1)
            dve.wait_ge(c_adj0, 16)
            dve.wait_ge(c_adj1, 16)
            for t in range(SUB):
                last = nc.vector.tensor_scalar(mask_b[:, t, :], adj_i[:, :], 0, MASKED, ALU.is_le, ALU.mult)
            last.then_inc(mask_ok, 1)

            def step(t, groups, q, m):
                g0, g1, gx, gl, gr = groups
                normed = g0 is not None or gx is not None
                if g0 is not None:
                    dve.wait_ge(x_in[q], 16 * (m + 1))
                if gr is not None:
                    dve.wait_ge(rank_ps, gr + 1)
                    nc.vector.tensor_tensor(rank[:, :, :], ps_rank.rearrange("p (t e) -> p t e", t=SUB),
                                            cst[:, C_BASE:C_TOKEN].rearrange("p (t e) -> p t e", t=SUB), ALU.add
                                            ).then_inc(rank_ok, 1)
                if g0 is not None:
                    for j in range(SUB):
                        last = nc.vector.bn_stats(bn[:, 0, j, :], x_all[:, bass.ds(g0, 1), j, :].rearrange("p g d -> p (g d)"))
                    last.then_inc(stats1_ok, 1)
                if gx is not None:
                    dve.wait_ge(hrelu_ok, gx + 1)
                    nc.vector.tensor_tensor(xr[:, :, :], hrelu[:, :, :],
                                            x_all[:, bass.ds(gx, 1), :, :].rearrange("p g s d -> p (g s) d"), ALU.add
                                            ).then_inc(xr_ok, 1)
                if gr is not None:
                    dve.wait_ge(rank_ok, gr + 1)
                    nc.vector.tensor_tensor(slot_p[:, :, :, :], chosen[:, :, :, :],
                                            rank[:, None, :, :].to_broadcast([P, 2, SUB, E]), ALU.mult
                                            ).then_inc(slotp_ok, 1)
                if g0 is not None:
                    dve.wait_ge(stats1_ok, g0 + 1)
                if gx is not None:
                    dve.wait_ge(hexp_ok, gx + 1)
                    nc.vector.tensor_scalar(u[:, :, :], hexp[:, :, :], 1.0, -1.0, ALU.min, ALU.add).then_inc(u_ok, 1)
                if g0 is not None:
                    for j in range(SUB):
                        last = nc.vector.bn_aggr(mv[:, 0, j, :], bn[:, 0, j, :])
                    last.then_inc(aggr1_ok, 1)
                if gx is not None:
                    dve.wait_ge(u_ok, gx + 1)
                    if later(m - 1):
                        dve.wait_ge(stored[q], 16 * (m - 1))
                    nc.vector.tensor_tensor(x2[q][:, :, :], xr[:, :, :], u[:, :, :], ALU.add).then_inc(x2_ok, 1)
                if gr is not None:
                    dve.wait_ge(slotp_ok, gr + 1)
                    if later(m - 2):
                        dve.wait_ge(rows_out[q], 16 * 2 * SUB * (m - 2))
                    with nc.allow_low_precision(reason="one term of a sum is a slot's number, the others are zero"):
                        nc.vector.tensor_reduce(slot_i[q][:, :], slot_p[:, :, :, :].rearrange("p k t e -> p (k t) e"),
                                                AX, ALU.add).then_inc(slot_ok, 1)
                if gx is not None:
                    dve.wait_ge(x2_ok, gx + 1)
                if g1 is not None:
                    dve.wait_ge(z_ok, g1 + 1)
                    nc.vector.scalar_tensor_tensor(score[:, :, :], z[:, :, :], SLOPE, z[:, :, :], ALU.mult, ALU.max
                                                   ).then_inc(score_ok, 1)
                if gx is not None:
                    for j in range(SUB):
                        last = nc.vector.bn_stats(bn[:, 1, j, :], x2[q][:, j, :])
                    last.then_inc(stats2_ok, 1)
                if g1 is not None:
                    dve.wait_ge(score_ok, g1 + 1)
                    nc.vector.tensor_reduce(smax[:, :], score[:, :, :], AX, ALU.max).then_inc(max_ok, 1)
                if gx is not None:
                    dve.wait_ge(stats2_ok, gx + 1)
                if gl is not None:
                    if later(gl):
                        dve.wait_ge(rowid_ok, gl)
                        dve.wait_ge(token_ok, gl)
                    nc.vector.tensor_scalar(token_f[:, :], token_f[:, :], float(GROUP), None, ALU.add).then_inc(token_ok, 1)
                if gx is not None:
                    for j in range(SUB):
                        last = nc.vector.bn_aggr(mv[:, 1, j, :], bn[:, 1, j, :])
                    last.then_inc(aggr2_ok, 1)
                if g1 is not None:
                    dve.wait_ge(max_ok, g1 + 1)
                    nc.vector.tensor_scalar(neg_max[:, :], smax[:, :], -1.0, None, ALU.mult).then_inc(neg_ok, 1)
                if normed:
                    if g0 is not None:
                        dve.wait_ge(aggr1_ok, g0 + 1)
                    if gx is not None:
                        dve.wait_ge(aggr2_ok, gx + 1)
                    nc.vector.tensor_scalar(var_eps[:, :], mv[:, :, :, 1].rearrange("p k j -> p (k j)"), EPS, None, ALU.add
                                            ).then_inc(var_ok, 1)
                if gl is not None:
                    if not later(gl):
                        dve.wait_ge(c_bg, 16)
                    dve.wait_ge(gate_ps, gl + 1)
                    nc.vector.tensor_tensor(logit[:, :, :], ps_gate.rearrange("p (t e) -> p t e", t=SUB),
                                            bg_sb[:, None, :].to_broadcast([P, SUB, E]), ALU.add).then_inc(logit_ok, 1)
                    dve.wait_ge(logit_ok, gl + 1)
                    if later(gl):
                        dve.wait_ge(seen_ok, 5 * gl)
                    nc.vector.tensor_copy(seen_b[:, 0, :], seen_b[:, SUB, :]).then_inc(seen_ok, 1)
                if gl is not None:
                    for j in range(SUB):
                        last = nc.vector.max(top[:, j, :], logit[:, j, :])
                    last.then_inc(top_ok, 1)
                    dve.wait_ge(top_ok, gl + 1)
                    nc.vector.tensor_tensor(gap[:, :], top[:, :, 1], top[:, :, 0], ALU.subtract).then_inc(gap_ok, 1)
                    for j in range(SUB):
                        last = nc.vector.max_index(top_i[:, j, :], top[:, j, :], logit[:, j, :])
                    last.then_inc(topi_ok, 1)
                    dve.wait_ge(topi_ok, gl + 1)
                    nc.vector.tensor_copy(top_f[:, :, :], top_i[:, :, 0:2].rearrange("p t k -> p k t")).then_inc(topf_ok, 1)
                    dve.wait_ge(topf_ok, gl + 1)
                    nc.vector.tensor_tensor(chosen[:, :, :, :], expert_no,
                                            top_f[:, :, :, None].to_broadcast([P, 2, SUB, E]), ALU.is_equal
                                            ).then_inc(chosen_ok, 1)
                if g0 is not None:
                    dve.wait_ge(rstd_ok, t + 1)
                    if later(g0):
                        dve.wait_ge(xn1_ps, g0)
                    for j in range(SUB):
                        nc.vector.tensor_scalar(xn1[:, j, :], x_all[:, bass.ds(g0, 1), j, :].rearrange("p g d -> p (g d)"),
                                                mv[:, 0, j, 0:1], rstd[:, j:j + 1], ALU.subtract, ALU.mult
                                                ).then_inc(xn1_ok, 1)
                if gl is not None:
                    dve.wait_ge(chosen_ok, gl + 1)
                    nc.vector.tensor_tensor(chosen_b[:, :, :], chosen[:, 0, :, :], chosen[:, 1, :, :], ALU.add
                                            ).then_inc(chosenb_ok, 1)
                if gx is not None:
                    dve.wait_ge(rstd_ok, t + 1)
                    if later(gx):
                        dve.wait_ge(xn2_ok, SUB * gx)
                    nc.vector.scalar_tensor_tensor(shift[:, :], mv[:, 1, :, 0], -1.0, rstd[:, SUB:2 * SUB], ALU.mult, ALU.mult
                                                   ).then_inc(shift_ok, 1)
                if gl is not None:
                    dve.wait_ge(gape_ok, gl + 1)
                    nc.vector.tensor_scalar(gap_1[:, :], gap_e[:, :], 1.0, None, ALU.add).then_inc(gap1_ok, 1)
                    for j in range(SUB):
                        if j == 0:
                            dve.wait_ge(chosenb_ok, gl + 1)
                        dve.wait_ge(seen_ok, 5 * gl + (1 + j))
                        nc.vector.tensor_tensor(seen_b[:, j + 1, :], seen_b[:, j, :], chosen_b[:, j, :], ALU.add
                                                ).then_inc(seen_ok, 1)
                if gl is not None:
                    dve.wait_ge(gap1_ok, gl + 1)
                    nc.vector.reciprocal(gate_p[:, 0, :], gap_1[:, :]).then_inc(p1_ok, 1)
                if g1 is not None:
                    dve.wait_ge(exp_ok, SUB * g1 + SUB)
                    if later(g1):
                        dve.wait_ge(hexp_ok, g1)
                    nc.vector.reciprocal(inv_sum[:, :], psum_row[:, :]).then_inc(inv_ok, 1)
                if gl is not None:
                    dve.wait_ge(p1_ok, gl + 1)
                    nc.vector.tensor_tensor(gate_p[:, 1, :], gap_e[:, :], gate_p[:, 0, :], ALU.mult).then_inc(p2_ok, 1)
                    if later(m + (q - 2)):
                        dve.wait_ge(rows_out[1 - q], 16 * 2 * SUB * (m + (q - 2)))
                    dve.wait_ge(token_ok, gl + 1)
                    nc.vector.tensor_copy(rows[1 - q][:, :, ID].bitcast(I32), token_f[:, :]).then_inc(rowid_ok, 1)
                    dve.wait_ge(p2_ok, gl + 1)
                    nc.vector.tensor_tensor(weighed[:, :, :, :], chosen[:, :, :, :],
                                            gate_p[:, :, :, None].to_broadcast([P, 2, SUB, E]), ALU.mult
                                            ).then_inc(weighed_ok, 1)
                    dve.wait_ge(weighed_ok, gl + 1)
                    nc.vector.tensor_tensor(rows[1 - q][:, :, D:ID], weighed[:, 0, :, :], weighed[:, 1, :, :], ALU.add
                                            ).then_inc(rowp_ok, 1)

            by_steps(dve, step)

            dve.wait_ge(count_ps, 1)
            nc.vector.tensor_copy(count_f[:, :], ps_count).then_inc(count_ok, 1)
            dve.wait_ge(count_ok, 1)
            nc.vector.tensor_copy(count_i[:, :], count_f[:, :])
            nc.vector.tensor_scalar(blocks_f[:, :], count_f[:, :], float(GROUP - 1), 1.0 / GROUP, ALU.add, ALU.mult
                                    ).then_inc(blocks_ok, 1)
            dve.wait_ge(blocks_ok, 1)
            nc.vector.tensor_scalar(blocks_i[:, :], blocks_f[:, :], 0.5 - 0.5 / GROUP, None, ALU.subtract).then_inc(blocks_ok, 1)
            dve.wait_ge(blocks_ok, 2)
            nc.vector.tensor_copy(blocks_r[:, :], blocks_i[:, :]).then_inc(blocks_ok, 1)
            dve.wait_ge(blocks_ok, 3)
            nc.vector.tensor_scalar(blocks_m[:, :], blocks_r[:, :], 1.0, None, ALU.max).then_inc(blocks_ok, 1)
            dve.wait_ge(blocks_ok, 4)
            nc.vector.tensor_tensor_scan(until_f[:, :], ones8[:, :], blocks_m[:, :], 0.0, ALU.mult, ALU.add).then_inc(blocks_ok, 1)
            dve.wait_ge(blocks_ok, 5)
            nc.vector.tensor_copy(until_i[:, :], until_f[:, :]).then_inc(table_ok, 1)
            for e in range(E):
                dve.wait_ge(hi_ok, e + 1)
                nc.vector.tensor_tensor(w1_lo[:, e, :], w1_raw[:, e, :], w1_hi[:, e, :].bitcast(F32), ALU.subtract)
                nc.vector.tensor_tensor(w2_lo[:, e, :, :], w2_raw[:, e, :, :], w2_hi[:, e, :, :].bitcast(F32), ALU.subtract
                                        ).then_inc(lo_ok, 1)
            bounds = block_bounds(dve)

            def low_x(i):
                dve.wait_ge(xh_ok, i + 1)
                nc.vector.tensor_tensor(xl[:, :], ps_x[:, :], xh[:, :].bitcast(F32), ALU.subtract).then_inc(xl_ok, 1)

            def keep_meta(i):
                dve.wait_ge(xs_in, 16 * (i + 1))
                dve.wait_ge(own_ok, i + FIRST)
                nc.vector.tensor_copy(meta[:, :, :], xs[:, :, D:ROW]).then_inc(meta_ok, 1)

            def weigh(i):
                parity = (i + 2) & 1
                dve.wait_ge(yt_ps, i + 2)
                for pair in range(2):
                    for t in (2 * pair, 2 * pair + 1):
                        dve.wait_ge(added[t], 16 * (i + 1))
                        nc.vector.tensor_scalar(ys[t][:, :], ps_yt[:, t * D:(t + 1) * D],
                                                wgt[:, bass.ds(parity, 1), t], None, ALU.mult)
                        last = nc.vector.tensor_copy(ysi[t][:, :], tid[:, bass.ds(parity, 1), t])
                    last.then_inc(ys_ok, 1)

            keep_meta(0)
            low_x(0)
            for e in range(E):
                with dve.Fori(bounds[e], bounds[e + 1]) as i:
                    dve.wait_ge(meta_ok, i + FIRST + 1)
                    dve.wait_ge(ys_ok, 2 * i + FIRST)
                    nc.vector.tensor_copy(wgt[:, bass.ds(i & 1, 1), :], meta[:, :, e:e + 1].rearrange("p t k -> p k t"))
                    nc.vector.tensor_copy(tid[:, bass.ds(i & 1, 1), :],
                                          meta[:, :, E:E + 1].rearrange("p t k -> p k t").bitcast(I32)).then_inc(own_ok, 1)
                    for c in range(HC):
                        if c % 2 == 0:
                            dve.wait_ge(r_ok, HC * i + (c + 1))
                            nc.vector.tensor_copy(hh[:, c, :], hr[:, c, :]).then_inc(hh_even_ok, 1)
                        if c == 0:
                            keep_meta(i + 1)
                        if c % 2 == 0:
                            dve.wait_ge(hh_even_ok, HC // 2 * i + (c // 2 + 1))
                        else:
                            dve.wait_ge(hh_odd_ok, HC // 2 * i + (c // 2 + 1))
                        nc.vector.tensor_tensor(hl[:, c, :], hr[:, c, :], hh[:, c, :].bitcast(F32), ALU.subtract
                                                ).then_inc(hl_ok, 1)
                    low_x(i + 1)
                    weigh(i - 1)
            dve.wait_ge(own_ok, bounds[E] + FIRST)
            weigh(bounds[E] - 1)

        @block.tensor
        def _(pe):
            pe.wait_ge(c_cst, 16)
            pe.wait_ge(c_wt, 16)
            pe.wait_ge(a_rep_ok, 1)
            nc.tensor.matmul(ps_setup[:, 0:P], wt_sb[:, :], a_rep[:, 0, :], start=True, stop=True).then_inc(xs_ps, FIRST)
            nc.tensor.matmul(ps_setup[:, P:2 * P], wt_sb[:, :], a_rep[:, 1, :], start=True, stop=True).then_inc(wa_ps, 1)

            def step(t, groups, q, m):
                g0, g1, gx, gl, _ = groups
                if g1 is not None:
                    if later(g1):
                        pe.wait_ge(prob_t_ok, g1)
                    for j in range(SUB):
                        pe.wait_ge(exp_ok, SUB * g1 + (j + 1))
                        last = nc.tensor.transpose(tiles(ps_tp)[:, j, :], prob[:, j, :], ident)
                    last.then_inc(prob_ps, 1)
                if g0 is not None:
                    if later(g0):
                        pe.wait_ge(xn1_t_ok, g0)
                    for j in range(SUB):
                        pe.wait_ge(xn1_ok, SUB * g0 + (j + 1))
                        last = nc.tensor.transpose(tiles(ps_t1)[:, j, :], xn1[:, j, :], ident)
                    last.then_inc(xn1_ps, 1)
                if g1 is not None:
                    pe.wait_ge(prob_t_ok, g1 + 1)
                    pe.wait_ge(wh_ok, g1 + 1)
                    if later(g1):
                        pe.wait_ge(hexp_ok, g1)
                    for j in range(SUB):
                        last = nc.tensor.matmul(tiles(ps_av)[:, j, :], prob_t[:, j, :], wh[:, j, :], start=True, stop=True)
                    last.then_inc(av_ps, 1)
                if gl is not None:
                    pe.wait_ge(seen_ok, 5 * gl + 5)
                    if later(gl):
                        pe.wait_ge(rank_ok, gl)
                    nc.tensor.matmul(ps_rank, before_b[:, :], chosen_b[:, :, :], start=True, stop=False)
                    nc.tensor.matmul(ps_rank, ones_b[:, :], seen_b[:, 0:SUB, :], start=False, stop=True).then_inc(rank_ps, 1)
                if g0 is not None:
                    pe.wait_ge(xn1_t_ok, g0 + 1)
                    if later(g0):
                        pe.wait_ge(z_ok, g0)
                    else:
                        pe.wait_ge(wa_ok, 1)
                        pe.wait_ge(mask_ok, 1)
                    nc.tensor.matmul(ps_z[:, :], ident_b[:, :], mask_b[:, :, :], start=True, stop=False)
                    nc.tensor.matmul(ps_z[:, :], w_a[:, 1, :], xn1_t[:, :], start=False, stop=False)
                    for j in range(SUB):
                        last = nc.tensor.matmul(tiles(ps_z)[:, j, :], xn1_t[:, j * P:(j + 1) * P], w_a[:, 0, :],
                                                start=False, stop=j == SUB - 1)
                    last.then_inc(z_ps, 1)
                if gx is not None:
                    if later(gx):
                        pe.wait_ge(xn2_t_ok, gx)
                    for j in range(SUB):
                        pe.wait_ge(xn2_ok, SUB * gx + (j + 1))
                        last = nc.tensor.transpose(tiles(ps_t3)[:, j, :], xn2[q][:, j, :], ident)
                    last.then_inc(xn2_ps, 1)
                if g0 is not None:
                    if later(g0):
                        pe.wait_ge(wh_ok, g0)
                    else:
                        pe.wait_ge(c_w, 16)
                    for j in range(SUB):
                        last = nc.tensor.matmul(tiles(ps_wh)[:, j, :], xn1_t[:, j * P:(j + 1) * P], w_sb[:, :],
                                                start=True, stop=True)
                    last.then_inc(wh_ps, 1)
                if gx is not None:
                    pe.wait_ge(xn2_t_ok, gx + 1)
                    if later(gx):
                        pe.wait_ge(logit_ok, gx)
                    else:
                        pe.wait_ge(c_wg, 16)
                    for j in range(SUB):
                        last = nc.tensor.matmul(ps_gate[:, j * E:(j + 1) * E], xn2_t[:, j * P:(j + 1) * P], wg_sb[:, :],
                                                start=True, stop=True)
                    last.then_inc(gate_ps, 1)

            by_steps(pe, step)
            pe.wait_ge(rank_ok, GROUPS)
            nc.tensor.matmul(ps_count, ones_b[:, :], seen_b[:, SUB, :], start=True, stop=True).then_inc(count_ps, 1)
            bounds = block_bounds(pe)

            def transpose_x(i):
                pe.wait_ge(xs_in, 16 * (i + 1))
                for t in range(SUB):
                    last = nc.tensor.transpose(ps_x[:, t * P:(t + 1) * P], xs[:, t, 0:D], ident)
                last.then_inc(xs_ps, 1)

            def transpose_y(i):
                pe.wait_ge(yb_ok, i + (FIRST + 1))
                pe.wait_ge(ys_ok, 2 * i + (2 + FIRST))
                for t in range(SUB):
                    last = nc.tensor.transpose(ps_yt[:, t * D:(t + 1) * D], yb[:, t * P:(t + 1) * P], ident)
                last.then_inc(yt_ps, 1)

            transpose_x(0)
            for e in range(E):
                pe.wait_ge(lo_ok, e + 1)
                with pe.Fori(bounds[e], bounds[e + 1]) as i:
                    pe.wait_ge(xl_ok, i + 1)
                    for c in range(HC):
                        chunk = slice(c * P, (c + 1) * P)
                        nc.tensor.matmul(ps_h[c][:, :], w1_hi[:, e, chunk], xh[:, :], start=True, stop=False)
                        nc.tensor.matmul(ps_h[c][:, :], w1_hi[:, e, chunk], xl[:, :], start=False, stop=False)
                        nc.tensor.matmul(ps_h[c][:, :], w1_lo[:, e, chunk], xh[:, :], start=False, stop=True
                                         ).then_inc(h_ps, 1)
                    transpose_x(i + 1)
                    transpose_y(i - 1)
                    for c in range(HC):
                        pe.wait_ge(hl_ok, HC * i + (c + 1))
                        nc.tensor.matmul(ps_y[:, :], w2_hi[:, e, c, :], hh[:, c, :], start=c == 0, stop=False)
                        nc.tensor.matmul(ps_y[:, :], w2_hi[:, e, c, :], hl[:, c, :], start=False, stop=False)
                        last = nc.tensor.matmul(ps_y[:, :], w2_lo[:, e, c, :], hh[:, c, :], start=False, stop=c == HC - 1)
                    last.then_inc(y_ps, 1)
            transpose_y(bounds[E] - 1)


def kernel(x, adj, L0_gnn_W, L0_gnn_a, L0_ffn_Wg, L0_ffn_bg, L0_ffn_W1, L0_ffn_b1, L0_ffn_W2, L0_ffn_b2):
    import numpy as np
    import concourse.bacc as bacc
    from concourse.bass_utils import run_bass_kernel_spmd

    def laid(v):
        return np.ascontiguousarray(v)

    w1, w2 = np.asarray(L0_ffn_W1), np.asarray(L0_ffn_W2)
    arrays = {
        "x": laid(np.asarray(x).reshape(TOKENS, D)),
        "adj": laid(np.asarray(adj)),
        "w": laid(np.asarray(L0_gnn_W)),
        "wt": laid(np.asarray(L0_gnn_W).T),
        "a": laid(np.asarray(L0_gnn_a).reshape(2, D).T),
        "wg_t": laid(np.asarray(L0_ffn_Wg).T),
        "bg": laid(np.asarray(L0_ffn_bg)),
        "w1_t": laid(w1.transpose(2, 0, 1)),
        "b1_t": laid(np.asarray(L0_ffn_b1).reshape(E, HC, P).transpose(2, 0, 1)),
        "w2_t": laid(w2.reshape(E, D, HC, P).transpose(3, 0, 2, 1)),
        "b2_t": laid(np.asarray(L0_ffn_b2).T),
        "consts": shape_constants(np),
    }
    nc = bacc.Bacc("TRN2", target_bir_lowering=False, num_devices=1)
    aps = {n: nc.dram_tensor(n, v.shape, mybir.dt.from_np(v.dtype), kind="ExternalInput").ap() for n, v in arrays.items()}
    out = nc.dram_tensor("out", (TOKENS + GROUP, D), F32, kind="ExternalOutput").ap()
    gnn_moe_kernel(nc, **aps, out=out)
    r = run_bass_kernel_spmd(nc, [arrays], core_ids=[0])
    return r.results[0]["out"][:TOKENS].reshape(128, NODES, D)
```

```python
import concourse.bass as bass
from concourse import mybir
from contextlib import ExitStack

F32 = mybir.dt.float32
F32R = mybir.dt.float32r
BF16 = mybir.dt.bfloat16
I32 = mybir.dt.int32
U32 = mybir.dt.uint32
ALU = mybir.AluOpType
ACT = mybir.ActivationFunctionType
AX = mybir.AxisListType.X

P = 128
NODES = 64
TOKENS = 128 * NODES
D = 128
H = 512
E = 8
SUB = 4
GROUP = SUB * P
GROUPS = TOKENS // GROUP
HC = H // P
WEIGHT, ID = D, D + 1
ROW = D + 2
CAP = TOKENS + GROUP
EPS = 1e-5
SLOPE = 0.2
BATCHES = [slice(0, 1), slice(1, 4), slice(4, 8), slice(8, 12), slice(12, GROUPS)]
BATCH = 4
STAGES = 5
MASKED = -1e30
META = 4
FIRST = 1

C_IDENT = 0
C_BEFORE = C_IDENT + P
C_EXPERT = C_BEFORE + P
C_BASE = C_EXPERT + 2 * SUB * E
C_TOKEN = C_BASE + SUB * E
C_PAD = C_TOKEN + SUB
C_END = C_PAD + SUB


def shape_constants(np):
    c = np.zeros((P, C_END), np.float32)
    c[:, C_IDENT:C_IDENT + P] = np.eye(P)
    c[:, C_BEFORE:C_BEFORE + P] = np.triu(np.ones((P, P)), 1)
    c[:, C_EXPERT:C_BASE] = np.tile(np.arange(E), 2 * SUB)
    c[:, C_BASE:C_TOKEN] = np.tile(np.arange(E) * CAP, SUB)
    c[:, C_TOKEN:C_PAD] = np.arange(SUB)[None, :] * P + np.arange(P)[:, None] - GROUP
    c[:, C_PAD:C_END] = TOKENS + np.arange(P)[:, None] * SUB + np.arange(SUB)[None, :]
    return c


def gnn_moe_kernel(nc, x, adj, w, wt, a, wg_t, bg, w1_t, b1_t, w2_t, b2_t, consts, out):
    ctx = ExitStack()
    with ctx:
        def sb(name, shape, dt=F32):
            return ctx.enter_context(nc.sbuf_tensor(name, shape, dt))

        def sem(name):
            return ctx.enter_context(nc.semaphore(name))

        slots = nc.dram_tensor("expert_slots", [E * CAP, ROW], F32, kind="Internal").ap()
        x_groups = x.rearrange("(g s p) d -> g p s d", s=SUB, p=P)
        out_groups = out[0:TOKENS, :].rearrange("(g s p) d -> g p s d", s=SUB, p=P)

        cst = sb("cst", [P, C_END])
        ident = cst[:, C_IDENT:C_IDENT + P]
        expert_no = cst[:, C_EXPERT:C_BASE].rearrange("p (k s e) -> p k s e", k=2, s=SUB)
        ident_b = sb("ident_b", [P, P], BF16)
        before_b = sb("before_b", [P, P], BF16)
        ones_b = sb("ones_b", [P, P], BF16)
        minus_half = sb("minus_half", [P, BATCH, SUB])
        act_scratch = sb("act_scratch", [P, 1])
        pool_scratch = sb("pool_scratch", [P, 1])
        w_sb = sb("w_sb", [P, D])
        wt_sb = sb("wt_sb", [P, D])
        a_sb = sb("a_sb", [P, 2])
        a_rep = sb("a_rep", [P, 2, P])
        w_a = sb("w_a", [P, 2, P])
        adj_i = sb("adj_i", [P, P], I32)
        mask_b = sb("mask_b", [P, SUB, P], BF16)
        wg_sb = sb("wg_sb", [P, E])
        bg_sb = sb("bg_sb", [P, E])
        b1_sb = sb("b1_sb", [P, E, HC])
        b2_sb = sb("b2_sb", [P, E])
        w1_raw = sb("w1_raw", [P, E, H])
        w2_raw = sb("w2_raw", [P, E, HC, D])
        w1_hi = sb("w1_hi", [P, E, H], F32R)
        w1_lo = sb("w1_lo", [P, E, H], F32R)
        w2_hi = sb("w2_hi", [P, E, HC, D], F32R)
        w2_lo = sb("w2_lo", [P, E, HC, D], F32R)
        pad_rows = sb("pad_rows", [P, SUB, ROW])

        x_all = sb("x_all", [P, GROUPS, SUB, D])
        bn1 = sb("bn1", [P, BATCH, SUB, 6])
        mv1 = sb("mv1", [P, GROUPS, SUB, 2])
        var1 = sb("var1", [P, GROUPS, SUB])
        rstd1 = sb("rstd1", [P, GROUPS, SUB])
        bn2 = sb("bn2", [P, SUB, 6])
        mv2 = sb("mv2", [P, SUB, 2])
        var2 = sb("var2", [P, SUB])
        rstd2 = sb("rstd2", [P, SUB])
        shift = sb("shift", [P, SUB])
        xn1 = sb("xn1", [P, SUB, D])
        xn1_t = sb("xn1_t", [P, GROUP])
        z = sb("z", [P, SUB, P])
        wh = sb("wh", [P, SUB, D])
        score = sb("score", [P, SUB, P])
        smax = sb("smax", [P, SUB])
        neg_max = sb("neg_max", [P, SUB])
        prob = sb("prob", [P, SUB, P])
        psum_row = sb("psum_row", [P, SUB])
        prob_t = sb("prob_t", [P, SUB, P])
        inv_sum = sb("inv_sum", [P, SUB])
        hrelu = sb("hrelu", [P, SUB, D])
        hexp = sb("hexp", [P, SUB, D])
        u = sb("u", [P, SUB, D])
        xr = sb("xr", [P, SUB, D])
        x2 = [sb(f"x2_{q}", [P, SUB, D]) for q in range(2)]
        xn2 = [sb(f"xn2_{q}", [P, SUB, D]) for q in range(2)]
        rows = [sb(f"rows{q}", [P, 2, SUB, ROW]) for q in range(2)]
        xn2_t = sb("xn2_t", [P, GROUP])
        logit = sb("logit", [P, SUB, E])
        top = sb("top", [P, SUB, 8])
        top_i = sb("top_i", [P, SUB, 8], U32)
        gap = sb("gap", [P, SUB])
        gap_e = sb("gap_e", [P, SUB])
        gap_1 = sb("gap_1", [P, SUB])
        top_f = sb("top_f", [P, 2, SUB])
        chosen = sb("chosen", [P, 2, SUB, E])
        chosen_b = sb("chosen_b", [P, SUB, E], BF16)
        seen_b = sb("seen_b", [P, SUB + 1, E], BF16)
        rank = sb("rank", [P, SUB, E])
        slot_p = sb("slot_p", [P, 2, SUB, E])
        slot_i = [sb(f"slot_i{q}", [P, 2 * SUB], I32) for q in range(2)]
        token_f = sb("token_f", [P, SUB])
        count_f = sb("count_f", [P, E])
        count_i = sb("count_i", [P, E], I32)
        blocks_f = sb("blocks_f", [P, E])
        blocks_i = sb("blocks_i", [P, E], I32)
        blocks_r = sb("blocks_r", [P, E])
        blocks_m = sb("blocks_m", [P, E])
        ones8 = sb("ones8", [P, E])
        until_f = sb("until_f", [P, E])
        until_i = sb("until_i", [P, E], I32)

        xs = sb("xs", [P, SUB, ROW])
        xh = sb("xh", [P, GROUP], F32R)
        xl = sb("xl", [P, GROUP], F32R)
        meta = sb("meta", [P, META, SUB, 2])
        hr = x_all[:, 0:HC, :, :].rearrange("p c s d -> p c (s d)")
        hh = sb("hh", [P, HC, GROUP], F32R)
        hl = sb("hl", [P, HC, GROUP], F32R)
        yb = sb("yb", [P, GROUP])
        ys = [sb(f"ys{s}", [P, D]) for s in range(SUB)]
        ysi = [sb(f"ysi{s}", [P, 1], I32) for s in range(SUB)]

        bank = [ctx.enter_context(nc.psum_tensor(f"bank{n}", [P, 512], F32)) for n in range(8)]
        ps_t1, ps_z, ps_wh, ps_tp, ps_av, ps_t3, ps_route, ps_setup = bank
        ps_gate, ps_rank, ps_count = ps_route[:, 0:SUB * E], ps_setup[:, 0:SUB * E], ps_setup[:, 64:64 + E]
        ps_h = bank[0:4]
        ps_x, ps_y, ps_yt = bank[4:7]

        c_w = sem("c_w")
        c_wt = sem("c_wt")
        c_a = sem("c_a")
        c_adj0 = sem("c_adj0")
        c_adj1 = sem("c_adj1")
        c_cst = sem("c_cst")
        c_wg = sem("c_wg")
        c_bg = sem("c_bg")
        c_b1 = sem("c_b1")
        c_b2 = sem("c_b2")
        c_w1 = sem("c_w1")
        c_w2 = sem("c_w2")
        int_zeros = sem("int_zeros")
        row_zeros = sem("row_zeros")
        start_ok = sem("start_ok")
        a_rep_ok = sem("a_rep_ok")
        wa_ps = sem("wa_ps")
        wa_ok = sem("wa_ok")
        mask_ok = sem("mask_ok")
        pads_ok = sem("pads_ok")
        hi_ok = sem("hi_ok")
        lo_ok = sem("lo_ok")
        stats1_ok = sem("stats1_ok")
        stats2_ok = sem("stats2_ok")
        aggr1_ok = sem("aggr1_ok")
        aggr2_ok = sem("aggr2_ok")
        var1_ok = sem("var1_ok")
        var2_ok = sem("var2_ok")
        rstd1_ok = sem("rstd1_ok")
        rstd2_ok = sem("rstd2_ok")
        shift_ok = sem("shift_ok")
        xn1_ok = sem("xn1_ok")
        xn1_ps = sem("xn1_ps")
        xn1_t_ok = sem("xn1_t_ok")
        z_ps = sem("z_ps")
        wh_ps = sem("wh_ps")
        z_ok = sem("z_ok")
        wh_ok = sem("wh_ok")
        score_ok = sem("score_ok")
        max_ok = sem("max_ok")
        neg_ok = sem("neg_ok")
        exp_ok = sem("exp_ok")
        prob_ps = sem("prob_ps")
        prob_t_ok = sem("prob_t_ok")
        av_ps = sem("av_ps")
        inv_ok = sem("inv_ok")
        hrelu_ok = sem("hrelu_ok")
        hexp_ok = sem("hexp_ok")
        xr_ok = sem("xr_ok")
        u_ok = sem("u_ok")
        x2_ok = sem("x2_ok")
        xn2_ok = sem("xn2_ok")
        xn2_ps = sem("xn2_ps")
        xn2_t_ok = sem("xn2_t_ok")
        gate_ps = sem("gate_ps")
        logit_ok = sem("logit_ok")
        top_ok = sem("top_ok")
        topi_ok = sem("topi_ok")
        gap_ok = sem("gap_ok")
        gape_ok = sem("gape_ok")
        gap1_ok = sem("gap1_ok")
        topf_ok = sem("topf_ok")
        p1_ok = sem("p1_ok")
        chosen_ok = sem("chosen_ok")
        chosenb_ok = sem("chosenb_ok")
        rowid_ok = sem("rowid_ok")
        rowx_ok = sem("rowx_ok")
        seen_ok = sem("seen_ok")
        rank_ps = sem("rank_ps")
        rank_ok = sem("rank_ok")
        slotp_ok = sem("slotp_ok")
        token_ok = sem("token_ok")
        slot_ok = sem("slot_ok")
        count_ps = sem("count_ps")
        count_ok = sem("count_ok")
        blocks_ok = sem("blocks_ok")
        table_ok = sem("table_ok")
        pads_out = sem("pads_out")
        xs_in = sem("xs_in")
        xs_ps = sem("xs_ps")
        xh_ok = sem("xh_ok")
        xl_ok = sem("xl_ok")
        meta_ok = sem("meta_ok")
        h_ps = sem("h_ps")
        r_ok = sem("r_ok")
        hh_even_ok = sem("hh_even_ok")
        hh_odd_ok = sem("hh_odd_ok")
        hl_ok = sem("hl_ok")
        y_ps = sem("y_ps")
        yb_ok = sem("yb_ok")
        yt_ps = sem("yt_ps")
        ys_ok = sem("ys_ok")
        dump_ok = sem("dump_ok")
        stood = sem("stood")
        x_in, rows_out, stored = ([sem(f"{n}{q}") for q in range(2)] for n in ("x_in", "rows_out", "stored"))
        added = [sem(f"added{t}") for t in range(SUB)]

        def tiles(ap):
            return ap[:, :].rearrange("p (t j) -> p t j", t=SUB)

        def later(n):
            return not isinstance(n, int) or n > 0

        def by_steps(eng, step):
            def at(t):
                step(t, [t - n if 0 <= t - n < GROUPS else None for n in range(STAGES)], t % 2, t // 2)

            for t in range(6):
                at(t)
            with eng.Fori(3, GROUPS // 2) as m:
                for q in range(2):
                    step(2 * m + q, [2 * m + (q - n) for n in range(STAGES)], q, m)
            for t in range(GROUPS, GROUPS + STAGES - 1):
                at(t)

        def block_bounds(eng):
            eng.wait_ge(table_ok, 1)
            return [0] + [eng.value_load(until_i[0:1, e:e + 1], min_val=1, max_val=TOKENS * 2 // GROUP + E)
                          for e in range(E)]

        block = ctx.enter_context(nc.Block())

        @block.sync
        def _(sp):
            sp.dma_start(a_sb[:, :], a).then_inc(c_a, 16)
            sp.dma_start(cst[:, :], consts).then_inc(c_cst, 16)
            sp.dma_start(x_all[:, 0, :, :], x_groups[0]).then_inc(x_in[0], 16)
            sp.dma_start(wt_sb[:, :], wt).then_inc(c_wt, 16)
            sp.wait_ge(int_zeros, 1)
            sp.dma_start(adj_i[0:NODES, 0:NODES], adj).then_inc(c_adj0, 16)
            sp.dma_start(adj_i[NODES:P, NODES:P], adj).then_inc(c_adj1, 16)
            sp.dma_start(w_sb[:, :], w).then_inc(c_w, 16)
            sp.dma_start(x_all[:, 1, :, :], x_groups[1]).then_inc(x_in[1], 16)
            sp.dma_start(wg_sb[:, :], wg_t).then_inc(c_wg, 16)
            sp.dma_start(bg_sb[:, :], bg.partition_broadcast(P)).then_inc(c_bg, 16)
            with sp.Fori(1, GROUPS // 2) as m:
                for q in range(2):
                    sp.wait_ge(x_in[q], 16 * m)
                    sp.dma_start(x_all[:, bass.ds(2 * m + q, 1), :, :],
                                 x_groups[bass.ds(2 * m + q, 1)].rearrange("g p s d -> p g s d")).then_inc(x_in[q], 16)
            sp.dma_start(w1_raw[:, :, :], w1_t).then_inc(c_w1, 16)
            sp.dma_start(w2_raw[:, :, :, :], w2_t).then_inc(c_w2, 16)
            sp.dma_start(b1_sb[:, :, :], b1_t).then_inc(c_b1, 16)
            sp.dma_start(b2_sb[:, :], b2_t).then_inc(c_b2, 16)
            sp.wait_ge(pads_ok, 1)
            sp.dma_start(out[TOKENS:TOKENS + GROUP, :].rearrange("(p s) d -> p s d", s=SUB),
                         pad_rows[:, :, 0:D]).then_inc(dump_ok, 16)

            def pass_on(m, q):
                g = 2 * m + q
                x2_due, xn2_due, scattered, passed = [v if isinstance(v, int) else nc.snap(v) for v in
                                                      (g + 1, SUB * g + SUB, 16 * 2 * SUB * m, 32 * g)]
                sp.wait_ge(x2_ok, x2_due)
                sp.dma_start(out_groups[bass.ds(g, 1)].rearrange("g p s d -> p g s d"),
                             x2[q][:, :, :].rearrange("p (g s) d -> p g s d", g=1)).then_inc(stored[q], 16)
                sp.wait_ge(xn2_ok, xn2_due)
                if later(m):
                    sp.wait_ge(rows_out[q], scattered)
                if later(g):
                    sp.wait_ge(rowx_ok, passed)
                for k in range(2):
                    sp.dma_start(rows[q][:, k, :, 0:D], xn2[q][:, :, :]).then_inc(rowx_ok, 16)

            for q in range(2):
                pass_on(0, q)
            with sp.Fori(1, GROUPS // 2) as m:
                for q in range(2):
                    pass_on(m, q)
            sp.wait_ge(table_ok, 1)
            for e in range(E):
                n = sp.value_load(count_i[0:1, e:e + 1], min_val=0, max_val=TOKENS)
                sp.dma_start(slots[bass.ds(n + e * CAP, GROUP), :].rearrange("(p s) r -> p s r", s=SUB),
                             pad_rows[:, :, :]).then_inc(pads_out, 16)
            bounds = block_bounds(sp)
            sp.wait_ge(pads_out, 16 * E)
            for q in range(2):
                sp.wait_ge(rows_out[q], 16 * 2 * SUB * (GROUPS // 2))

            def load_block(first_row, i):
                sp.wait_ge(xs_ps, i + FIRST)
                sp.wait_ge(meta_ok, i + FIRST)
                sp.dma_start(xs[:, :, :], slots[bass.ds(first_row, GROUP), :].rearrange("(p s) r -> p s r", s=SUB)
                             ).then_inc(xs_in, 16)

            for e in range(E):
                with sp.Fori(bounds[e], bounds[e + 1]) as i:
                    row = nc.s_assert_within((i - bounds[e]) * GROUP + e * CAP, e * CAP, (e + 1) * CAP - GROUP,
                                             skip_runtime_bounds_check_because="an expert has at most TOKENS tokens")
                    load_block(row, i)
            load_block(0, bounds[E])
            for q in range(2):
                sp.wait_ge(stored[q], 16 * (GROUPS // 2))

        def stand(pool, before):
            pool.wait_ge(stood, before + FIRST)
            nc.gpsimd.tensor_tensor(pool_scratch[:, :], minus_half[:, 0, 0:1], minus_half[:, 0, 0:1], ALU.add
                                    ).then_inc(stood, 1)

        @block.gpsimd
        def _(pool):
            nc.gpsimd.memset(adj_i[:, :], 0).then_inc(int_zeros, 1)
            nc.gpsimd.memset(minus_half[:, :, :], -0.5).then_inc(stood, FIRST)
            nc.gpsimd.memset(pad_rows[:, :, :], 0.0).then_inc(row_zeros, 1)
            pool.wait_ge(c_cst, 16)
            pool.wait_ge(row_zeros, 1)
            nc.gpsimd.tensor_copy(pad_rows[:, :, ID], cst[:, C_PAD:C_END]).then_inc(pads_ok, 1)

            def first_rstd(b):
                n = BATCHES[b].stop - BATCHES[b].start
                pool.wait_ge(var1_ok, b + 1)
                nc.gpsimd.tensor_tensor(rstd1[:, BATCHES[b], :], var1[:, BATCHES[b], :], minus_half[:, 0:n, :], ALU.pow
                                        ).then_inc(rstd1_ok, 1)

            def step(t, groups, q, m):
                _, _, gx, _, gr = groups
                if isinstance(t, int) and t == 0:
                    first_rstd(0)
                if gx is not None:
                    pool.wait_ge(var2_ok, gx + 1)
                    if later(gx):
                        pool.wait_ge(xn2_ok, SUB * gx)
                    nc.gpsimd.tensor_tensor(rstd2[:, :], var2[:, :], minus_half[:, 0, :], ALU.pow).then_inc(rstd2_ok, 1)
                if isinstance(t, int) and t + 1 < len(BATCHES):
                    first_rstd(t + 1)
                if gr is not None:
                    pool.wait_ge(slot_ok, gr + 1)
                    pool.wait_ge(rowx_ok, 32 * (gr + 1))
                    stand(pool, gr)
                    for k in range(2):
                        for j in range(SUB):
                            nc.gpsimd.indirect_dma_start(
                                out=slots, out_offset=bass.IndirectOffsetOnAxis(
                                    ap=slot_i[q][:, k * SUB + j:k * SUB + j + 1], axis=0),
                                in_=rows[q][:, k, j, :], in_offset=None).then_inc(rows_out[q], 16)

            by_steps(pool, step)
            bounds = block_bounds(pool)
            for q in range(2):
                pool.wait_ge(stored[q], 16 * (GROUPS // 2))
            pool.wait_ge(dump_ok, 16)

            def add_rows(i, experts):
                for t in range(SUB):
                    if t % 2 == 0:
                        pool.wait_ge(ys_ok, 2 * (i + 1) + (FIRST + 1 + t // 2))
                        stand(pool, GROUPS + experts + 2 * (i + 1) + t // 2)
                    nc.gpsimd.indirect_dma_start(
                        out=out, out_offset=bass.IndirectOffsetOnAxis(ap=ysi[t][:, :], axis=0),
                        in_=ys[t][:, :], in_offset=None, compute_op=ALU.add).then_inc(added[t], 16)

            add_rows(-1, 0)
            for e in range(E):
                for t in range(SUB):
                    pool.wait_ge(added[t], bounds[e] * 16 + 16)
                stand(pool, GROUPS + e + 2 * (bounds[e] + 1))
                with pool.Fori(bounds[e], bounds[e + 1]) as i:
                    add_rows(i, e + 1)
            for t in range(SUB):
                pool.wait_ge(added[t], bounds[E] * 16 + 16)

        @block.scalar
        def _(act):
            act.wait_ge(c_cst, 16)
            nc.scalar.copy(act_scratch[:, :], cst[:, 0:1]).then_inc(yb_ok, FIRST)
            act.wait_ge(wa_ps, 1)
            nc.scalar.copy(w_a[:, :, :], ps_setup[:, 0:2 * P].rearrange("p (k j) -> p k j", k=2)).then_inc(wa_ok, 1)

            def step(t, groups, q, m):
                g0, g1, gx, gl, _ = groups
                if g1 is not None:
                    act.wait_ge(neg_ok, g1 + 1)
                    if later(g1):
                        act.wait_ge(prob_ps, g1)
                    for j in range(SUB):
                        nc.scalar.activation(prob[:, j, :], score[:, j, :], ACT.Exp, bias=neg_max[:, j:j + 1],
                                             accum_out=psum_row[:, j:j + 1]).then_inc(exp_ok, 1)
                if g1 is not None:
                    act.wait_ge(prob_ps, g1 + 1)
                    if later(g1):
                        act.wait_ge(av_ps, g1)
                    nc.scalar.copy(prob_t[:, :, :], tiles(ps_tp)).then_inc(prob_t_ok, 1)
                if g0 is not None:
                    act.wait_ge(xn1_ps, g0 + 1)
                    if later(g0):
                        act.wait_ge(wh_ps, g0)
                    nc.scalar.copy(xn1_t[:, :], ps_t1[:, :]).then_inc(xn1_t_ok, 1)
                if gl is not None:
                    act.wait_ge(gap_ok, gl + 1)
                    nc.scalar.activation(gap_e[:, :], gap[:, :], ACT.Exp).then_inc(gape_ok, 1)
                if g1 is not None:
                    act.wait_ge(av_ps, g1 + 1)
                    act.wait_ge(inv_ok, g1 + 1)
                    if later(g1):
                        act.wait_ge(xr_ok, g1)
                        act.wait_ge(u_ok, g1)
                    for j in range(SUB):
                        last = nc.scalar.activation(hrelu[:, j, :], tiles(ps_av)[:, j, :], ACT.Relu, scale=inv_sum[:, j:j + 1])
                    last.then_inc(hrelu_ok, 1)
                    for j in range(SUB):
                        last = nc.scalar.activation(hexp[:, j, :], tiles(ps_av)[:, j, :], ACT.Exp, scale=inv_sum[:, j:j + 1])
                    last.then_inc(hexp_ok, 1)
                if g0 is not None:
                    act.wait_ge(z_ps, g0 + 1)
                    if later(g0):
                        act.wait_ge(score_ok, g0)
                    nc.scalar.copy(z[:, :, :], tiles(ps_z)).then_inc(z_ok, 1)
                if gx is not None:
                    act.wait_ge(shift_ok, gx + 1)
                    if later(gx - 1):
                        act.wait_ge(rowx_ok, 32 * (gx - 1))
                    for j in range(SUB):
                        nc.scalar.activation(xn2[q][:, j, :], x2[q][:, j, :], ACT.Identity, bias=shift[:, j:j + 1],
                                             scale=rstd2[:, j:j + 1]).then_inc(xn2_ok, 1)
                if gx is not None:
                    act.wait_ge(xn2_ps, gx + 1)
                    if later(gx):
                        act.wait_ge(gate_ps, gx)
                    nc.scalar.copy(xn2_t[:, :], ps_t3[:, :]).then_inc(xn2_t_ok, 1)
                if g0 is not None:
                    act.wait_ge(wh_ps, g0 + 1)
                    nc.scalar.copy(wh[:, :, :], tiles(ps_wh)).then_inc(wh_ok, 1)

            by_steps(act, step)
            act.wait_ge(c_w1, 16)
            act.wait_ge(c_w2, 16)
            for e in range(E):
                nc.scalar.copy(w1_hi[:, e, :], w1_raw[:, e, :])
                nc.scalar.copy(w2_hi[:, e, :, :], w2_raw[:, e, :, :]).then_inc(hi_ok, 1)
            bounds = block_bounds(act)
            act.wait_ge(c_b1, 16)
            act.wait_ge(c_b2, 16)

            def round_x(i):
                act.wait_ge(xs_ps, i + FIRST + 1)
                nc.scalar.copy(xh[:, :], ps_x[:, :]).then_inc(xh_ok, 1)

            round_x(0)
            for e in range(E):
                with act.Fori(bounds[e], bounds[e + 1]) as i:
                    for c in range(HC):
                        act.wait_ge(h_ps, HC * i + (c + 1))
                        nc.scalar.activation(hr[:, c, :], ps_h[c][:, :], ACT.Relu, bias=b1_sb[:, e, c:c + 1]
                                             ).then_inc(r_ok, 1)
                        if c % 2:
                            nc.scalar.activation(hh[:, c, :], ps_h[c][:, :], ACT.Relu, bias=b1_sb[:, e, c:c + 1]
                                                 ).then_inc(hh_odd_ok, 1)
                    round_x(i + 1)
                    act.wait_ge(y_ps, i + 1)
                    nc.scalar.activation(yb[:, :], ps_y[:, :], ACT.Identity, bias=b2_sb[:, e:e + 1]
                                         ).then_inc(yb_ok, 1)

        @block.vector
        def _(dve):
            nc.vector.memset(ones_b[:, :], 1.0)
            nc.vector.memset(ones8[:, :], 1.0).then_inc(meta_ok, FIRST)
            nc.vector.memset(yb[:, :], 0.0).then_inc(ys_ok, FIRST)
            nc.vector.memset(meta[:, :, :, :], 0.0)
            nc.vector.memset(seen_b[:, :, :], 0.0).then_inc(start_ok, 1)
            dve.wait_ge(c_cst, 16)
            nc.vector.tensor_copy(ident_b[:, :], ident)
            nc.vector.tensor_copy(before_b[:, :], cst[:, C_BEFORE:C_BEFORE + P])
            nc.vector.tensor_copy(token_f[:, :], cst[:, C_TOKEN:C_PAD])
            dve.wait_ge(start_ok, 1)
            nc.vector.tensor_copy(meta[:, META - 1, :, 1], cst[:, C_PAD:C_END])
            dve.wait_ge(c_a, 16)
            for k in range(2):
                last = nc.vector.tensor_scalar(a_rep[:, k, :], ones_b[:, :], a_sb[:, k:k + 1], None, ALU.mult)
            last.then_inc(a_rep_ok, 1)
            dve.wait_ge(c_adj0, 16)
            dve.wait_ge(c_adj1, 16)
            for t in range(SUB):
                last = nc.vector.tensor_scalar(mask_b[:, t, :], adj_i[:, :], 0, MASKED, ALU.is_le, ALU.mult)
            last.then_inc(mask_ok, 1)

            def first_stats(b):
                for g in range(BATCHES[b].start, BATCHES[b].stop):
                    dve.wait_ge(x_in[g % 2], 16 * (g // 2 + 1))
                    for j in range(SUB):
                        last = nc.vector.bn_stats(bn1[:, g - BATCHES[b].start, j, :], x_all[:, g, j, :])
                last.then_inc(stats1_ok, 1)
                dve.wait_ge(stats1_ok, b + 1)
                for g in range(BATCHES[b].start, BATCHES[b].stop):
                    for j in range(SUB):
                        last = nc.vector.bn_aggr(mv1[:, g, j, :], bn1[:, g - BATCHES[b].start, j, :])
                last.then_inc(aggr1_ok, 1)
                dve.wait_ge(aggr1_ok, b + 1)
                nc.vector.tensor_scalar(var1[:, BATCHES[b], :], mv1[:, BATCHES[b], :, 1], EPS, None, ALU.add).then_inc(var1_ok, 1)

            def step(t, groups, q, m):
                g0, g1, gx, gl, gr = groups
                if isinstance(t, int) and t == 0:
                    first_stats(0)
                if gr is not None:
                    dve.wait_ge(rank_ps, gr + 1)
                    nc.vector.tensor_tensor(rank[:, :, :], ps_rank.rearrange("p (t e) -> p t e", t=SUB),
                                            cst[:, C_BASE:C_TOKEN].rearrange("p (t e) -> p t e", t=SUB), ALU.add
                                            ).then_inc(rank_ok, 1)
                if gx is not None:
                    dve.wait_ge(hrelu_ok, gx + 1)
                    nc.vector.tensor_tensor(xr[:, :, :], hrelu[:, :, :],
                                            x_all[:, bass.ds(gx, 1), :, :].rearrange("p g s d -> p (g s) d"), ALU.add
                                            ).then_inc(xr_ok, 1)
                if gr is not None:
                    dve.wait_ge(rank_ok, gr + 1)
                    nc.vector.tensor_tensor(slot_p[:, :, :, :], chosen[:, :, :, :],
                                            rank[:, None, :, :].to_broadcast([P, 2, SUB, E]), ALU.mult
                                            ).then_inc(slotp_ok, 1)
                if gx is not None:
                    dve.wait_ge(hexp_ok, gx + 1)
                    nc.vector.tensor_scalar(u[:, :, :], hexp[:, :, :], 1.0, -1.0, ALU.min, ALU.add).then_inc(u_ok, 1)
                if gx is not None:
                    dve.wait_ge(u_ok, gx + 1)
                    if later(m - 1):
                        dve.wait_ge(stored[q], 16 * (m - 1))
                    nc.vector.tensor_tensor(x2[q][:, :, :], xr[:, :, :], u[:, :, :], ALU.add).then_inc(x2_ok, 1)
                if gr is not None:
                    dve.wait_ge(slotp_ok, gr + 1)
                    if later(m - 2):
                        dve.wait_ge(rows_out[q], 16 * 2 * SUB * (m - 2))
                    with nc.allow_low_precision(reason="one term of a sum is a slot's number, the others are zero"):
                        nc.vector.tensor_reduce(slot_i[q][:, :], slot_p[:, :, :, :].rearrange("p k t e -> p (k t) e"),
                                                AX, ALU.add).then_inc(slot_ok, 1)
                if gx is not None:
                    dve.wait_ge(x2_ok, gx + 1)
                if g1 is not None:
                    dve.wait_ge(z_ok, g1 + 1)
                    nc.vector.scalar_tensor_tensor(score[:, :, :], z[:, :, :], SLOPE, z[:, :, :], ALU.mult, ALU.max
                                                   ).then_inc(score_ok, 1)
                if g1 is not None:
                    dve.wait_ge(score_ok, g1 + 1)
                    nc.vector.tensor_reduce(smax[:, :], score[:, :, :], AX, ALU.max).then_inc(max_ok, 1)
                for j in range(SUB):
                    if gx is not None:
                        last = nc.vector.bn_stats(bn2[:, j, :], x2[q][:, j, :])
                        if j == SUB - 1:
                            last.then_inc(stats2_ok, 1)
                    if j == 0 and g1 is not None:
                        dve.wait_ge(max_ok, g1 + 1)
                        nc.vector.tensor_scalar(neg_max[:, :], smax[:, :], -1.0, None, ALU.mult).then_inc(neg_ok, 1)
                if gx is not None:
                    dve.wait_ge(stats2_ok, gx + 1)
                if gl is not None:
                    if later(gl):
                        dve.wait_ge(rowid_ok, gl)
                        dve.wait_ge(token_ok, gl)
                    nc.vector.tensor_scalar(token_f[:, :], token_f[:, :], float(GROUP), None, ALU.add).then_inc(token_ok, 1)
                if gx is not None:
                    for j in range(SUB):
                        last = nc.vector.bn_aggr(mv2[:, j, :], bn2[:, j, :])
                    last.then_inc(aggr2_ok, 1)
                if gx is not None:
                    dve.wait_ge(aggr2_ok, gx + 1)
                    nc.vector.tensor_scalar(var2[:, :], mv2[:, :, 1], EPS, None, ALU.add).then_inc(var2_ok, 1)
                if g0 is not None:
                    if not later(t - 6):
                        dve.wait_ge(rstd1_ok, 1 + sum(g0 >= batch.start for batch in BATCHES[1:]))
                    if later(g0):
                        dve.wait_ge(xn1_ps, g0)
                    for j in range(SUB):
                        nc.vector.tensor_scalar(xn1[:, j, :], x_all[:, bass.ds(g0, 1), j, :].rearrange("p g d -> p (g d)"),
                                                mv1[:, bass.ds(g0, 1), j, 0], rstd1[:, bass.ds(g0, 1), j],
                                                ALU.subtract, ALU.mult
                                                ).then_inc(xn1_ok, 1)
                if gl is not None:
                    if not later(gl):
                        dve.wait_ge(c_bg, 16)
                    dve.wait_ge(gate_ps, gl + 1)
                    nc.vector.tensor_tensor(logit[:, :, :], ps_gate.rearrange("p (t e) -> p t e", t=SUB),
                                            bg_sb[:, None, :].to_broadcast([P, SUB, E]), ALU.add).then_inc(logit_ok, 1)
                    dve.wait_ge(logit_ok, gl + 1)
                    if later(gl):
                        dve.wait_ge(seen_ok, 5 * gl)
                    nc.vector.tensor_copy(seen_b[:, 0, :], seen_b[:, SUB, :]).then_inc(seen_ok, 1)
                if gl is not None:
                    for j in range(SUB):
                        last = nc.vector.max(top[:, j, :], logit[:, j, :])
                    last.then_inc(top_ok, 1)
                    dve.wait_ge(top_ok, gl + 1)
                    nc.vector.tensor_tensor(gap[:, :], top[:, :, 1], top[:, :, 0], ALU.subtract).then_inc(gap_ok, 1)
                    for j in range(SUB):
                        last = nc.vector.max_index(top_i[:, j, :], top[:, j, :], logit[:, j, :])
                    last.then_inc(topi_ok, 1)
                    dve.wait_ge(topi_ok, gl + 1)
                    nc.vector.tensor_copy(top_f[:, :, :], top_i[:, :, 0:2].rearrange("p t k -> p k t")).then_inc(topf_ok, 1)
                    dve.wait_ge(topf_ok, gl + 1)
                    nc.vector.tensor_tensor(chosen[:, :, :, :], expert_no,
                                            top_f[:, :, :, None].to_broadcast([P, 2, SUB, E]), ALU.is_equal
                                            ).then_inc(chosen_ok, 1)
                if g1 is not None:
                    dve.wait_ge(exp_ok, SUB * g1 + SUB)
                    if later(g1):
                        dve.wait_ge(hexp_ok, g1)
                    nc.vector.reciprocal(inv_sum[:, :], psum_row[:, :]).then_inc(inv_ok, 1)
                if gl is not None:
                    dve.wait_ge(chosen_ok, gl + 1)
                    nc.vector.tensor_tensor(chosen_b[:, :, :], chosen[:, 0, :, :], chosen[:, 1, :, :], ALU.add
                                            ).then_inc(chosenb_ok, 1)
                if gx is not None:
                    dve.wait_ge(rstd2_ok, gx + 1)
                    if later(gx):
                        dve.wait_ge(xn2_ok, SUB * gx)
                    nc.vector.scalar_tensor_tensor(shift[:, :], mv2[:, :, 0], -1.0, rstd2[:, :], ALU.mult, ALU.mult
                                                   ).then_inc(shift_ok, 1)
                if gl is not None:
                    dve.wait_ge(gape_ok, gl + 1)
                    nc.vector.tensor_scalar(gap_1[:, :], gap_e[:, :], 1.0, None, ALU.add).then_inc(gap1_ok, 1)
                    for j in range(SUB):
                        if j == 0:
                            dve.wait_ge(chosenb_ok, gl + 1)
                        dve.wait_ge(seen_ok, 5 * gl + (1 + j))
                        nc.vector.tensor_tensor(seen_b[:, j + 1, :], seen_b[:, j, :], chosen_b[:, j, :], ALU.add
                                                ).then_inc(seen_ok, 1)
                if gl is not None:
                    if later(m + (q - 2)):
                        dve.wait_ge(rows_out[1 - q], 16 * 2 * SUB * (m + (q - 2)))
                    dve.wait_ge(gap1_ok, gl + 1)
                    nc.vector.reciprocal(rows[1 - q][:, 0, :, WEIGHT], gap_1[:, :]).then_inc(p1_ok, 1)
                    dve.wait_ge(p1_ok, gl + 1)
                    nc.vector.tensor_tensor(rows[1 - q][:, 1, :, WEIGHT], gap_e[:, :], rows[1 - q][:, 0, :, WEIGHT], ALU.mult)
                    dve.wait_ge(token_ok, gl + 1)
                    nc.vector.tensor_copy(rows[1 - q][:, :, :, ID], token_f[:, None, :].to_broadcast([P, 2, SUB])).then_inc(rowid_ok, 1)
                if isinstance(t, int) and t + 1 < len(BATCHES):
                    first_stats(t + 1)

            by_steps(dve, step)

            dve.wait_ge(count_ps, 1)
            nc.vector.tensor_copy(count_f[:, :], ps_count).then_inc(count_ok, 1)
            dve.wait_ge(count_ok, 1)
            nc.vector.tensor_copy(count_i[:, :], count_f[:, :])
            nc.vector.tensor_scalar(blocks_f[:, :], count_f[:, :], float(GROUP - 1), 1.0 / GROUP, ALU.add, ALU.mult
                                    ).then_inc(blocks_ok, 1)
            dve.wait_ge(blocks_ok, 1)
            nc.vector.tensor_scalar(blocks_i[:, :], blocks_f[:, :], 0.5 - 0.5 / GROUP, None, ALU.subtract).then_inc(blocks_ok, 1)
            dve.wait_ge(blocks_ok, 2)
            nc.vector.tensor_copy(blocks_r[:, :], blocks_i[:, :]).then_inc(blocks_ok, 1)
            dve.wait_ge(blocks_ok, 3)
            nc.vector.tensor_scalar(blocks_m[:, :], blocks_r[:, :], 1.0, None, ALU.max).then_inc(blocks_ok, 1)
            dve.wait_ge(blocks_ok, 4)
            nc.vector.tensor_tensor_scan(until_f[:, :], ones8[:, :], blocks_m[:, :], 0.0, ALU.mult, ALU.add).then_inc(blocks_ok, 1)
            dve.wait_ge(blocks_ok, 5)
            nc.vector.tensor_copy(until_i[:, :], until_f[:, :]).then_inc(table_ok, 1)
            for e in range(E):
                dve.wait_ge(hi_ok, e + 1)
                nc.vector.tensor_tensor(w1_lo[:, e, :], w1_raw[:, e, :], w1_hi[:, e, :].bitcast(F32), ALU.subtract)
                nc.vector.tensor_tensor(w2_lo[:, e, :, :], w2_raw[:, e, :, :], w2_hi[:, e, :, :].bitcast(F32), ALU.subtract
                                        ).then_inc(lo_ok, 1)
            bounds = block_bounds(dve)

            def low_x(i):
                dve.wait_ge(xh_ok, i + 1)
                nc.vector.tensor_tensor(xl[:, :], ps_x[:, :], xh[:, :].bitcast(F32), ALU.subtract).then_inc(xl_ok, 1)

            def keep_meta(i):
                dve.wait_ge(xs_in, 16 * (i + 1))
                nc.vector.tensor_copy(meta[:, bass.ds(i & (META - 1), 1), :, :].rearrange("p n t k -> p (n t) k"),
                                      xs[:, :, WEIGHT:ROW]).then_inc(meta_ok, 1)

            def weigh(i):
                kept = (i + META) & (META - 1)
                dve.wait_ge(meta_ok, i + FIRST + 1)
                dve.wait_ge(yt_ps, i + 2)
                for t in range(SUB):
                    dve.wait_ge(added[t], 16 * (i + 1))
                    nc.vector.tensor_scalar(ys[t][:, :], ps_yt[:, t * D:(t + 1) * D],
                                            meta[:, bass.ds(kept, 1), t, 0], None, ALU.mult)
                    last = nc.vector.tensor_copy(ysi[t][:, :], meta[:, bass.ds(kept, 1), t, 1])
                    if t % 2:
                        last.then_inc(ys_ok, 1)

            keep_meta(0)
            low_x(0)
            for e in range(E):
                with dve.Fori(bounds[e], bounds[e + 1]) as i:
                    dve.wait_ge(ys_ok, 2 * i + FIRST)
                    for c in range(HC):
                        if c % 2 == 0:
                            dve.wait_ge(r_ok, HC * i + (c + 1))
                            nc.vector.tensor_copy(hh[:, c, :], hr[:, c, :]).then_inc(hh_even_ok, 1)
                        if c == 0:
                            keep_meta(i + 1)
                        if c % 2 == 0:
                            dve.wait_ge(hh_even_ok, HC // 2 * i + (c // 2 + 1))
                        else:
                            dve.wait_ge(hh_odd_ok, HC // 2 * i + (c // 2 + 1))
                        nc.vector.tensor_tensor(hl[:, c, :], hr[:, c, :], hh[:, c, :].bitcast(F32), ALU.subtract
                                                ).then_inc(hl_ok, 1)
                    low_x(i + 1)
                    weigh(i - 1)
            weigh(bounds[E] - 1)

        @block.tensor
        def _(pe):
            pe.wait_ge(c_cst, 16)
            pe.wait_ge(c_wt, 16)
            pe.wait_ge(a_rep_ok, 1)
            nc.tensor.matmul(ps_setup[:, 0:P], wt_sb[:, :], a_rep[:, 0, :], start=True, stop=True).then_inc(xs_ps, FIRST)
            nc.tensor.matmul(ps_setup[:, P:2 * P], wt_sb[:, :], a_rep[:, 1, :], start=True, stop=True).then_inc(wa_ps, 1)

            def step(t, groups, q, m):
                g0, g1, gx, gl, _ = groups
                if g1 is not None:
                    if later(g1):
                        pe.wait_ge(prob_t_ok, g1)
                    for j in range(SUB):
                        pe.wait_ge(exp_ok, SUB * g1 + (j + 1))
                        last = nc.tensor.transpose(tiles(ps_tp)[:, j, :], prob[:, j, :], ident)
                    last.then_inc(prob_ps, 1)
                if g0 is not None:
                    if later(g0):
                        pe.wait_ge(xn1_t_ok, g0)
                    for j in range(SUB):
                        pe.wait_ge(xn1_ok, SUB * g0 + (j + 1))
                        last = nc.tensor.transpose(tiles(ps_t1)[:, j, :], xn1[:, j, :], ident)
                    last.then_inc(xn1_ps, 1)
                if g1 is not None:
                    pe.wait_ge(prob_t_ok, g1 + 1)
                    pe.wait_ge(wh_ok, g1 + 1)
                    if later(g1):
                        pe.wait_ge(hexp_ok, g1)
                    for j in range(SUB):
                        last = nc.tensor.matmul(tiles(ps_av)[:, j, :], prob_t[:, j, :], wh[:, j, :], start=True, stop=True)
                    last.then_inc(av_ps, 1)
                if gl is not None:
                    pe.wait_ge(seen_ok, 5 * gl + 5)
                    if later(gl):
                        pe.wait_ge(rank_ok, gl)
                    nc.tensor.matmul(ps_rank, before_b[:, :], chosen_b[:, :, :], start=True, stop=False)
                    nc.tensor.matmul(ps_rank, ones_b[:, :], seen_b[:, 0:SUB, :], start=False, stop=True).then_inc(rank_ps, 1)
                if g0 is not None:
                    pe.wait_ge(xn1_t_ok, g0 + 1)
                    if later(g0):
                        pe.wait_ge(z_ok, g0)
                    else:
                        pe.wait_ge(wa_ok, 1)
                        pe.wait_ge(mask_ok, 1)
                    nc.tensor.matmul(ps_z[:, :], ident_b[:, :], mask_b[:, :, :], start=True, stop=False)
                    nc.tensor.matmul(ps_z[:, :], w_a[:, 1, :], xn1_t[:, :], start=False, stop=False)
                    for j in range(SUB):
                        last = nc.tensor.matmul(tiles(ps_z)[:, j, :], xn1_t[:, j * P:(j + 1) * P], w_a[:, 0, :],
                                                start=False, stop=j == SUB - 1)
                    last.then_inc(z_ps, 1)
                if gx is not None:
                    if later(gx):
                        pe.wait_ge(xn2_t_ok, gx)
                    for j in range(SUB):
                        pe.wait_ge(xn2_ok, SUB * gx + (j + 1))
                        last = nc.tensor.transpose(tiles(ps_t3)[:, j, :], xn2[q][:, j, :], ident)
                    last.then_inc(xn2_ps, 1)
                if g0 is not None:
                    if later(g0):
                        pe.wait_ge(wh_ok, g0)
                    else:
                        pe.wait_ge(c_w, 16)
                    for j in range(SUB):
                        last = nc.tensor.matmul(tiles(ps_wh)[:, j, :], xn1_t[:, j * P:(j + 1) * P], w_sb[:, :],
                                                start=True, stop=True)
                    last.then_inc(wh_ps, 1)
                if gx is not None:
                    pe.wait_ge(xn2_t_ok, gx + 1)
                    if later(gx):
                        pe.wait_ge(logit_ok, gx)
                    else:
                        pe.wait_ge(c_wg, 16)
                    for j in range(SUB):
                        last = nc.tensor.matmul(ps_gate[:, j * E:(j + 1) * E], xn2_t[:, j * P:(j + 1) * P], wg_sb[:, :],
                                                start=True, stop=True)
                    last.then_inc(gate_ps, 1)

            by_steps(pe, step)
            pe.wait_ge(rank_ok, GROUPS)
            nc.tensor.matmul(ps_count, ones_b[:, :], seen_b[:, SUB, :], start=True, stop=True).then_inc(count_ps, 1)
            bounds = block_bounds(pe)

            def transpose_x(i):
                pe.wait_ge(xs_in, 16 * (i + 1))
                for t in range(SUB):
                    last = nc.tensor.transpose(ps_x[:, t * P:(t + 1) * P], xs[:, t, 0:D], ident)
                last.then_inc(xs_ps, 1)

            def transpose_y(i):
                pe.wait_ge(yb_ok, i + (FIRST + 1))
                pe.wait_ge(ys_ok, 2 * i + (2 + FIRST))
                for t in range(SUB):
                    last = nc.tensor.transpose(ps_yt[:, t * D:(t + 1) * D], yb[:, t * P:(t + 1) * P], ident)
                last.then_inc(yt_ps, 1)

            transpose_x(0)
            for e in range(E):
                pe.wait_ge(lo_ok, e + 1)
                with pe.Fori(bounds[e], bounds[e + 1]) as i:
                    pe.wait_ge(xh_ok, i + 1)
                    for c in range(HC):
                        chunk = slice(c * P, (c + 1) * P)
                        nc.tensor.matmul(ps_h[c][:, :], w1_hi[:, e, chunk], xh[:, :], start=True, stop=False)
                        nc.tensor.matmul(ps_h[c][:, :], w1_lo[:, e, chunk], xh[:, :], start=False, stop=False)
                        if c == 0:
                            pe.wait_ge(xl_ok, i + 1)
                        nc.tensor.matmul(ps_h[c][:, :], w1_hi[:, e, chunk], xl[:, :], start=False, stop=True
                                         ).then_inc(h_ps, 1)
                    transpose_x(i + 1)
                    transpose_y(i - 1)
                    for c in range(HC):
                        if c % 2 == 0:
                            pe.wait_ge(hh_even_ok, HC // 2 * i + (c // 2 + 1))
                        else:
                            pe.wait_ge(hh_odd_ok, HC // 2 * i + (c // 2 + 1))
                        nc.tensor.matmul(ps_y[:, :], w2_hi[:, e, c, :], hh[:, c, :], start=c == 0, stop=False)
                        nc.tensor.matmul(ps_y[:, :], w2_lo[:, e, c, :], hh[:, c, :], start=False, stop=False)
                        pe.wait_ge(hl_ok, HC * i + (c + 1))
                        last = nc.tensor.matmul(ps_y[:, :], w2_hi[:, e, c, :], hl[:, c, :], start=False, stop=c == HC - 1)
                    last.then_inc(y_ps, 1)
            transpose_y(bounds[E] - 1)


def kernel(x, adj, L0_gnn_W, L0_gnn_a, L0_ffn_Wg, L0_ffn_bg, L0_ffn_W1, L0_ffn_b1, L0_ffn_W2, L0_ffn_b2):
    import numpy as np
    import concourse.bacc as bacc
    from concourse.bass_utils import run_bass_kernel_spmd

    def laid(v):
        return np.ascontiguousarray(v)

    w1, w2 = np.asarray(L0_ffn_W1), np.asarray(L0_ffn_W2)
    arrays = {
        "x": laid(np.asarray(x).reshape(TOKENS, D)),
        "adj": laid(np.asarray(adj)),
        "w": laid(np.asarray(L0_gnn_W)),
        "wt": laid(np.asarray(L0_gnn_W).T),
        "a": laid(np.asarray(L0_gnn_a).reshape(2, D).T),
        "wg_t": laid(np.asarray(L0_ffn_Wg).T),
        "bg": laid(np.asarray(L0_ffn_bg)),
        "w1_t": laid(w1.transpose(2, 0, 1)),
        "b1_t": laid(np.asarray(L0_ffn_b1).reshape(E, HC, P).transpose(2, 0, 1)),
        "w2_t": laid(w2.reshape(E, D, HC, P).transpose(3, 0, 2, 1)),
        "b2_t": laid(np.asarray(L0_ffn_b2).T),
        "consts": shape_constants(np),
    }
    nc = bacc.Bacc("TRN2", target_bir_lowering=False, num_devices=1)
    aps = {n: nc.dram_tensor(n, v.shape, mybir.dt.from_np(v.dtype), kind="ExternalInput").ap() for n, v in arrays.items()}
    out = nc.dram_tensor("out", (TOKENS + GROUP, D), F32, kind="ExternalOutput").ap()
    gnn_moe_kernel(nc, **aps, out=out)
    r = run_bass_kernel_spmd(nc, [arrays], core_ids=[0])
    return r.results[0]["out"][:TOKENS].reshape(128, NODES, D)
```
